# Optimizing a Trainium2 kernel written in Bass

```python
import numpy as np
import jax
import jax.numpy as jnp

def _softmax(x, axis=-1):
    return jax.nn.softmax(x, axis=axis)

def _gelu(x):
    return jax.nn.gelu(x, approximate=True)

def _silu(x):
    return jax.nn.silu(x)

def _sigmoid(x):
    return jax.nn.sigmoid(x)

def _layernorm(x, axis=-1, eps=1e-05):
    m = jnp.mean(x, axis=axis, keepdims=True)
    v = jnp.var(x, axis=axis, keepdims=True)
    return (x - m) / jnp.sqrt(v + eps)

def _scatter_add(tgt, idx, src, axis=0):
    return tgt.at[idx].add(src)

def _segment_sum(src, seg, n):
    return jax.ops.segment_sum(src, seg, n)
kernel_name = 'mk_flamingo_gated_d1_seqx_r8_4d8fa7'

def setup_inputs(seed: int=0):
    np.random.seed(seed)
    _w = jnp.asarray

    def _rec_inputs():
        import jax
        import jax.numpy as jnp
        _rk = jax.random.key(seed)
        x = -0.0005207 + 1.001 * jax.random.normal(jax.random.fold_in(_rk, 1), (16, 256, 128), jnp.float32)
        _lenS = 256 - jax.random.randint(jax.random.fold_in(_rk, 7), (16,), 0, max(1, 256 // 4) + 1, jnp.int32)
        _lenS2 = 1601 - jax.random.randint(jax.random.fold_in(_rk, 8), (16,), 0, max(1, 1601 // 4) + 1, jnp.int32)
        _ctx_1024P = jax.random.normal(jax.random.fold_in(_rk, 11), (16, 16, 128), jnp.float32)
        _ctx_1024c = jax.random.dirichlet(jax.random.fold_in(_rk, 511), 0.3 * jnp.ones((16,), jnp.float32), (16, 1601))
        _ctx_1024t = jnp.einsum('bsk,bkd->bsd', _ctx_1024c, _ctx_1024P)
        _ctx_1024t = _ctx_1024t * jax.lax.rsqrt(jnp.mean(jnp.square(_ctx_1024t)) + 1e-12) * 0.953939
        ctx_1024 = -1.39393e-06 + 0.999914 * (_ctx_1024t + 0.3 * jax.random.normal(jax.random.fold_in(_rk, 611), (16, 1601, 128), jnp.float32))
        _validS = jnp.arange(256)[None, :] < _lenS[:, None]
        _validS2 = jnp.arange(1601)[None, :] < _lenS2[:, None]
        _causal = jnp.tril(jnp.ones((256, 256), dtype=bool))
        mask_BxS2_bf1 = jnp.ones((16, 1601), dtype=bool)
        _g = jax.random.normal(jax.random.fold_in(_rk, 9001), (2, 1), jnp.float32)
        _g = jnp.sign(_g) * jnp.maximum(jnp.abs(_g), 1.0) + (_g == 0) * 1.0
        g_xattn = _g[0]
        g_ffn = _g[1]
        return (x, ctx_1024, mask_BxS2_bf1, g_xattn, g_ffn)
    x, ctx_1024, mask_BxS2_bf1, g_xattn, g_ffn = _rec_inputs()

    def _L0_xattn_setup():
        import jax, jax.numpy as jnp
        import numpy as np
        B, M, N = (2, 128, 256)
        D_MODEL = 128
        H, HKV, D = (16, 4, 64)
        GROUPS = H // HKV
        THETA = 10000.0
        MAX_REL = M + N

        def _freqs_cis(dim, seq_len, theta):
            inv = 1.0 / theta ** (jnp.arange(0, dim, 2, dtype=jnp.float32) / dim)
            f = jnp.outer(jnp.arange(seq_len, dtype=jnp.float32), inv)
            f = jnp.repeat(f, 2, axis=-1)
            return (jnp.cos(f), jnp.sin(f))

        def _apply_rope(x, cos, sin):
            cos = cos[None, None]
            sin = sin[None, None]
            d = x.shape[-1]
            x1, x2 = (x[..., :d // 2], x[..., d // 2:])
            c1, c2 = (cos[..., :d // 2], cos[..., d // 2:])
            s1, s2 = (sin[..., :d // 2], sin[..., d // 2:])
            return jnp.concatenate([x1 * c1 - x2 * s1, x1 * s2 + x2 * c2], axis=-1)
        key = jax.random.key(seed)
        ks = jax.random.split(key, 8)
        sc = lambda fan_in: 1.0 / np.sqrt(fan_in)
        return {'q': jax.random.normal(ks[0], (B, M, D_MODEL), jnp.float32), 'kv': jax.random.normal(ks[1], (B, N, D_MODEL), jnp.float32), 'Wq': jax.random.normal(ks[2], (D_MODEL, H * D), jnp.float32) * sc(D_MODEL), 'Wk': jax.random.normal(ks[3], (D_MODEL, HKV * D), jnp.float32) * sc(D_MODEL), 'Wv': jax.random.normal(ks[4], (D_MODEL, HKV * D), jnp.float32) * sc(D_MODEL), 'Wo': jax.random.normal(ks[5], (H * D, D_MODEL), jnp.float32) * sc(H * D), 'rel_pos_bias': jnp.zeros((H, MAX_REL), jnp.float32), 'mask': jnp.ones((B, N), dtype=bool)}
    _L0_xattn_all = _L0_xattn_setup()
    _L0_xattn_in = {k: v for k, v in _L0_xattn_all.items() if k in ('Wq', 'Wk', 'Wv', 'Wo', 'rel_pos_bias')}
    del _L0_xattn_all

    def _L0_ffn_setup():
        import jax, jax.numpy as jnp
        import numpy as np
        EMBED_DIM = 128
        HIDDEN_DIM = 512
        NUM_EXPERTS = 8
        TOP_K = 2
        key = jax.random.key(seed)
        k_x, k_g, k_w1, k_w2 = jax.random.split(key, 4)
        x = jax.random.normal(k_x, (2, 64, EMBED_DIM), dtype=jnp.float32)
        gate_w = jax.random.normal(k_g, (NUM_EXPERTS, EMBED_DIM), dtype=jnp.float32) * (1.0 / np.sqrt(EMBED_DIM))
        w1 = jax.random.normal(k_w1, (NUM_EXPERTS, EMBED_DIM, HIDDEN_DIM), dtype=jnp.float32) * np.sqrt(2.0 / EMBED_DIM)
        b1 = jnp.zeros((NUM_EXPERTS, HIDDEN_DIM), dtype=jnp.float32)
        w2 = jax.random.normal(k_w2, (NUM_EXPERTS, HIDDEN_DIM, EMBED_DIM), dtype=jnp.float32) * np.sqrt(2.0 / HIDDEN_DIM)
        b2 = jnp.zeros((NUM_EXPERTS, EMBED_DIM), dtype=jnp.float32)
        return {'x': x, 'gate_w': gate_w, 'w1': w1, 'b1': b1, 'w2': w2, 'b2': b2}
    _L0_ffn_all = _L0_ffn_setup()
    _L0_ffn_in = {k: v for k, v in _L0_ffn_all.items() if k in ('gate_w', 'w1', 'b1', 'w2', 'b2')}
    del _L0_ffn_all
    return {'x': x, 'ctx_1024': ctx_1024, 'mask_BxS2_bf1': mask_BxS2_bf1, 'g_xattn': g_xattn, 'g_ffn': g_ffn, 'L0_xattn_Wq': _L0_xattn_in['Wq'], 'L0_xattn_Wk': _L0_xattn_in['Wk'], 'L0_xattn_Wv': _L0_xattn_in['Wv'], 'L0_xattn_Wo': _L0_xattn_in['Wo'], 'L0_xattn_rel_pos_bias': _L0_xattn_in['rel_pos_bias'], 'L0_ffn_gate_w': _L0_ffn_in['gate_w'], 'L0_ffn_w1': _L0_ffn_in['w1'], 'L0_ffn_b1': _L0_ffn_in['b1'], 'L0_ffn_w2': _L0_ffn_in['w2'], 'L0_ffn_b2': _L0_ffn_in['b2']}

def reference(x, ctx_1024, mask_BxS2_bf1, g_xattn, g_ffn, L0_xattn_Wq, L0_xattn_Wk, L0_xattn_Wv, L0_xattn_Wo, L0_xattn_rel_pos_bias, L0_ffn_gate_w, L0_ffn_w1, L0_ffn_b1, L0_ffn_w2, L0_ffn_b2):
    import jax
    import jax.numpy as jnp

    def _L0_xattn_ref(q, kv, Wq, Wk, Wv, Wo, rel_pos_bias, mask):
        import jax, jax.numpy as jnp
        import numpy as np
        B, M, N = (2, 128, 256)
        D_MODEL = 128
        H, HKV, D = (16, 4, 64)
        GROUPS = H // HKV
        THETA = 10000.0
        MAX_REL = M + N

        def _freqs_cis(dim, seq_len, theta):
            inv = 1.0 / theta ** (jnp.arange(0, dim, 2, dtype=jnp.float32) / dim)
            f = jnp.outer(jnp.arange(seq_len, dtype=jnp.float32), inv)
            f = jnp.repeat(f, 2, axis=-1)
            return (jnp.cos(f), jnp.sin(f))

        def _apply_rope(x, cos, sin):
            cos = cos[None, None]
            sin = sin[None, None]
            d = x.shape[-1]
            x1, x2 = (x[..., :d // 2], x[..., d // 2:])
            c1, c2 = (cos[..., :d // 2], cos[..., d // 2:])
            s1, s2 = (sin[..., :d // 2], sin[..., d // 2:])
            return jnp.concatenate([x1 * c1 - x2 * s1, x1 * s2 + x2 * c2], axis=-1)
        Bq, Mq, _ = q.shape
        Nk = kv.shape[1]
        Q = (q @ Wq).reshape(Bq, Mq, H, D).transpose(0, 2, 1, 3)
        K = (kv @ Wk).reshape(Bq, Nk, HKV, D).transpose(0, 2, 1, 3)
        V = (kv @ Wv).reshape(Bq, Nk, HKV, D).transpose(0, 2, 1, 3)
        cos_q, sin_q = _freqs_cis(D, Mq, THETA)
        cos_k, sin_k = _freqs_cis(D, Nk, THETA)
        Q = _apply_rope(Q, cos_q, sin_q)
        K = _apply_rope(K, cos_k, sin_k)
        K = jnp.repeat(K, GROUPS, axis=1)
        V = jnp.repeat(V, GROUPS, axis=1)
        scale = D ** (-0.5)
        scores = jnp.einsum('bhqd,bhkd->bhqk', Q, K) * scale
        rel = jnp.abs(jnp.arange(Mq)[:, None] - jnp.arange(Nk)[None, :])
        rel = jnp.clip(rel, 0, MAX_REL - 1)
        scores = scores + rel_pos_bias[:, rel][None]
        m = mask[:, None, None, :]
        scores = jnp.where(m, scores, -1000000000.0)
        attn = jax.nn.softmax(scores, axis=-1)
        out = jnp.einsum('bhqk,bhkd->bhqd', attn, V)
        out = out.transpose(0, 2, 1, 3).reshape(Bq, Mq, H * D)
        return out @ Wo

    def _L0_ffn_ref(x, gate_w, w1, b1, w2, b2):
        import jax, jax.numpy as jnp
        import numpy as np
        EMBED_DIM = 128
        HIDDEN_DIM = 512
        NUM_EXPERTS = 8
        TOP_K = 2
        orig_shape = x.shape
        xt = x.reshape(-1, EMBED_DIM)
        logits = xt @ gate_w.T
        probs = jax.nn.softmax(logits, axis=-1)
        top_w, top_i = jax.lax.top_k(probs, TOP_K)
        top_w = top_w / (top_w.sum(axis=-1, keepdims=True) + 1e-09)
        h = jnp.einsum('td,ndh->tnh', xt, w1) + b1
        h = jax.nn.gelu(h, approximate=False)
        out_all = jnp.einsum('tnh,nhd->tnd', h, w2) + b2
        sel = jnp.take_along_axis(out_all, top_i[:, :, None], axis=1)
        out = (sel * top_w[:, :, None]).sum(axis=1)
        return out.reshape(orig_shape)
    x = x + jnp.tanh(g_xattn[0]) * _L0_xattn_ref(_layernorm(x, axis=-1), ctx_1024, L0_xattn_Wq, L0_xattn_Wk, L0_xattn_Wv, L0_xattn_Wo, L0_xattn_rel_pos_bias, mask_BxS2_bf1)
    x = x + jnp.tanh(g_ffn[0]) * _L0_ffn_ref(_layernorm(x, axis=-1), L0_ffn_gate_w, L0_ffn_w1, L0_ffn_b1, L0_ffn_w2, L0_ffn_b2)
    return x

_drawn_inputs = setup_inputs


def setup_inputs(seed=0):
    import zlib

    import numpy as np

    out = dict(_drawn_inputs(seed))
    spreads = {'L0_xattn_rel_pos_bias': (0.0, 0.302), 'L0_ffn_b1': (0.0, 0.1), 'L0_ffn_b2': (0.0, 0.1)}
    factors = {}
    for name, (base, spread) in spreads.items():
        noise = np.random.default_rng([zlib.crc32(name.encode()), seed]).standard_normal(out[name].shape)
        drawn = base * np.exp(spread * noise) if base else spread * noise
        out[name] = jnp.asarray(drawn.astype(out[name].dtype))
    for name, factor in factors.items():
        out[name] = (out[name] * factor).astype(out[name].dtype)
    return out
```

```python
import concourse.bass as bass
from concourse import mybir
from contextlib import ExitStack

B, M, S2, DM = 16, 256, 1601, 128
H, HKV, D = 16, 4, 64
G = H // HKV
QT = M // 128
KT = (S2 + 127) // 128
KP = KT * 128
UNITS = B * HKV
UC = G * M
MAXREL = 384
NEAR = 5
WIN = (NEAR - 1) * 128 + M
ERING = 4
NE, HID, TOPC = 8, 512, 2
HC = HID // 128
TT = B * QT
TG = 4
BIG_Q, BIG_K = 32768.0, -30528.0
CHUNKS = [(0, 320, True), (320, 320, True), (640, 481, False), (1121, 480, False)]
NCH = len(CHUNKS)
PA = G * QT * NCH
PA_STEPS = [3, 3, 3, 3, 2, 3, 3, 3, 3, 3, 3, 0, 0]
assert sum(PA_STEPS) == PA and len(PA_STEPS) == KT
PA_FROM = [sum(PA_STEPS[:t]) for t in range(KT + 1)]
KV_ROUNDS = [(r, min(4, KT - r)) for r in range(0, KT, 4)]
KTR = [(0, 8), (8, KT - 8)]


class Unit:

    def __init__(self, reg, c):
        self.reg, self.c = reg, c
        self.g = c % HKV

    def at(self, d):
        return Unit(self.reg, self.c + d)

    def count(self, k, off=0):
        c = k * self.c + off
        return c if self.reg is None else self.reg * (HKV * k) + c

    def batch(self, k=1, off=0):
        c = k * (self.c // HKV) + off
        return c if self.reg is None else self.reg * k + c

    def is_at_most(self, last):
        return self.reg is not None or self.c <= last

    def is_at_least(self, first):
        return self.reg is not None or self.c >= first


def flamingo_block(nc, x, ctxT, mask, g_x, g_f, wq, wkv, wo2, bias_f, bias_far, gateT, w1, b1T, w2, b2,
                   rope_k, rope_q, ident_in, out):
    F32, F16 = mybir.dt.float32, mybir.dt.float16
    ALU = mybir.AluOpType
    ACT = mybir.ActivationFunctionType
    AX = mybir.AxisListType
    ds = bass.ds
    mb_dram = nc.dram_tensor("mask_bias", [B, KP], F16, kind="Internal").ap()
    ctx = ExitStack()
    with ctx:
        def sb(name, shape, dt=F32):
            return ctx.enter_context(nc.sbuf_tensor(name, shape, dt))

        def ps(name, cols):
            return ctx.enter_context(nc.psum_tensor(name, [128, cols], F32))

        def sem(name):
            return ctx.enter_context(nc.semaphore(name))

        X = sb("X", [128, TT, DM])
        WB = sb("WB", [128, H, WIN])
        K1 = sb("K1", [128, HKV, KP], F16)
        K2 = sb("K2", [128, HKV, KP], F16)
        Q1 = sb("Q1", [128, HKV, UC], F16)
        Q2 = sb("Q2", [128, HKV, UC], F16)
        V = sb("V", [128, HKV, KT, D])
        E = sb("E", [128, ERING, UC])
        esum = sb("esum", [128, 2, UC])
        ctx_sb = sb("ctx_sb", [128, KP])
        kr = sb("kr", [128, KT, D])
        kt1 = sb("kt1", [128, 4, D])
        kt2 = sb("kt2", [128, 4, D])
        khl = sb("khl", [128, KT, 2 * D], F16)
        qr = sb("qr", [128, QT, G, D])
        qt1 = sb("qt1", [128, QT, G, D])
        qt2 = sb("qt2", [128, QT, G, D])
        qhl = sb("qhl", [128, QT, G, 2 * D], F16)
        oraw = sb("oraw", [128, 512])
        rden = sb("rden", [128, 512])
        wkv_sb = sb("wkv_sb", [128, HKV, 2 * D])
        wq_sb = sb("wq_sb", [128, H * D])
        wo_sb = sb("wo_sb", [128, HKV * 2, DM])
        rk = sb("rk", [128, KT, 2, D])
        rkm = sb("rkm", [128, KT, 2, D])
        rq = sb("rq", [128, QT, 2, D])
        xn = sb("xn", [128, TG, DM])
        xnT = sb("xnT", [128, M])
        ident = sb("ident", [128, 128])
        ident16 = sb("ident16", [128, 128], F16)
        ones = sb("ones", [128, 128])
        maskT = sb("maskT", [128, B, KT])
        anyb = sb("anyb", [128, B])
        any16 = sb("any16", [B, 1])
        diag16 = sb("diag16", [B, B])
        mb16 = sb("mb16", [B, KP], F16)
        far = sb("far", [128, H])
        pm = sb("pm", [128, G * QT, NCH])
        mred = sb("mred", [128, G * QT])
        m16 = sb("m16", [128, G * QT], F16)
        mT = sb("mT", [G * QT, 128], F16)
        junk = sb("junk", [128, 2, 320])
        stats = sb("stats", [128, TT, 6])
        mv = sb("mv", [128, TT, 2])
        std = sb("std", [128, TT])
        rstd = sb("rstd", [128, TT])
        gx = sb("gx", [128, 2])
        tg_ = sb("tg_", [128, 2])
        gate_sb = sb("gate_sb", [128, NE])
        b1_sb = sb("b1_sb", [128, NE * HC])
        iota_r = sb("iota_r", [128, NE])
        r1 = sb("r1", [128, TT])
        r2 = sb("r2", [128, TT])
        r3 = sb("r3", [128, TT])
        onorm = oraw
        Vf = V[:, :, :, :].rearrange("p g t d -> p (g t d)")
        onerow = Vf[0:1, 0:KP // 2].bitcast(F16)
        bigrow = Vf[0:1, KP // 2:KP // 2 + UC // 2].bitcast(F16)
        mask_u8 = Vf[0:B, 1400:1400 + (S2 + 3) // 4].bitcast(mybir.dt.uint8)[:, 0:S2]
        lg, pr, ga, gb, wsel = (Vf[:, i * TT * NE:(i + 1) * TT * NE].rearrange("p (t e) -> p t e", e=NE)
                                for i in range(5))
        b2_sb = Vf[:, 2048:2048 + NE * DM].rearrange("p (e d) -> p e d", e=NE)
        mask_f = E[0:B, 0:2, :].rearrange("p a c -> p (a c)")[:, 0:KP]
        mask_t = E[0:B, 2:4, :].rearrange("p a c -> p (a c)")[:, 0:KP]
        WBf = WB[:, :, :].rearrange("p h w -> p (h w)")
        W1 = WBf[:, 0:NE * HID]
        W2 = WBf[:, NE * HID:2 * NE * HID]
        XT2 = WBf[:, 2 * NE * HID:2 * NE * HID + TT * 128]
        hid = E[:, :, :].rearrange("p r c -> p (r c)")
        oe = esum[:, :, :].rearrange("p a c -> p (a c)")
        xTs = ctx_sb[:, 0:512]

        stp = [ps(f"st{i}", UC) for i in range(2)]
        pap = [ps(f"pa{i}", 512) for i in range(2)]
        op = ps("op", 512)
        mp = ps("mp", 512)
        mp16 = mp[:, :].bitcast(F16)
        mp_kv = mp[:, :].rearrange("p (t c) -> p t c", t=4)

        names = """mb_out const_in x_in ctx_in mrow_in rows_in bias_in ffw_in out_done
            init_pool init_dve ident_up mask_f_up mask_ps mask_sb any_up any_ps any_sb mb_up bias_up
            var_up std_up rstd_up tanh_up rkm_up xn_up xt_ps xnT_sb kv_ps v_sb k_rope kh_up kl_up
            kt_ps k2_sb k1_sb q_ps q_rope qh_up ql_up qt_ps q2_sb q1_sb zrow
            pa_ps pa_seen pa_max pm_red m16_up mt_ps mT_sb st_ps bias_done e_up pv_ps sum_up o_sb den_ps
            rden_up on_up wo_ps y_up
            f_stats f_std f_rstd f_xn f_xt_ps f_xT_act f_xT_dve f_lg_ps f_lg f_sub f_exp f_gate
            f_h_ps f_gelu f_o_ps f_ob f_y""".split()
        s = {n: sem(n) for n in names}
        mbrow_in = [sem(f"mbrow_in{g}") for g in range(HKV)]
        block = ctx.enter_context(nc.Block())

        N_CONST = 11

        @block.sync
        def _(sp):
            sp.dma_start(X[:, :, :], x.rearrange("b (q p) d -> p (b q) d", p=128)).then_inc(s["x_in"], 16)
            sp.dma_start(mask_u8[:, :], mask).then_inc(s["x_in"], 16)
            for dst, src in ((ident[:, :], ident_in), (wkv_sb[:, :, :], wkv), (wq_sb[:, :], wq),
                             (rk[:, :, :, :], rope_k), (rq[:, :, :, :], rope_q), (wo_sb[:, :, :], wo2),
                             (gx[:, 0:1], g_x.partition_broadcast(128)), (gx[:, 1:2], g_f.partition_broadcast(128)),
                             (gate_sb[:, :], gateT), (b1_sb[:, :], b1T),
                             (far[:, :], bias_far.partition_broadcast(128))):
                sp.dma_start(dst, src).then_inc(s["const_in"], 16)
            sp.wait_ge(s["init_pool"], 1)
            sp.dma_start(ctx_sb[:, 0:S2], ctxT[0, :, :]).then_inc(s["ctx_in"], 16)
            sp.dma_start(WB[:, :, :], bass.AP(tensor=bias_f.tensor, offset=bias_f.offset,
                                              ap=[[1, 128], [bias_f.shape[1], H], [1, WIN]])).then_inc(s["bias_in"], 16)
            sp.wait_ge(s["init_pool"], 5)
            for g in range(HKV):
                sp.dma_start(K1[D:D + 1, g, :], onerow[:, :]).then_inc(s["rows_in"], 16)
                sp.dma_start(Q1[D + 1:D + 2, g, :], bigrow[:, :]).then_inc(s["rows_in"], 16)

            def mask_row(P):
                if P.is_at_least(HKV):
                    sp.wait_ge(s["st_ps"], P.count(KT, -3 * KT))
                sp.dma_start(K1[D + 1:D + 2, P.g, :], mb_dram[ds(P.batch(), 1), :]).then_inc(mbrow_in[P.g], 16)

            def max_row(A):
                sp.wait_ge(s["mT_sb"], A.count(1, 1))
                sp.dma_start(Q1[D:D + 1, A.g, :].rearrange("o (a b) -> o a b", b=128), mT[:, :])\
                  .then_inc(s["mrow_in"], 16)

            def unit(u):
                if u.g == 1 and u.is_at_most(UNITS - 4):
                    sp.wait_ge(s["kv_ps"], u.count(4, 4 * 3))
                    sp.dma_start(ctx_sb[:, 0:S2], ctxT[ds(u.batch(1, 1), 1), :, :].rearrange("o d k -> (o d) k"))\
                      .then_inc(s["ctx_in"], 16)
                if u.is_at_most(UNITS - 4):
                    mask_row(u.at(3))
                if u.is_at_most(UNITS - 2):
                    max_row(u.at(1))

            sp.wait_ge(s["mb_up"], 3)
            sp.dma_start(mb_dram, mb16[:, :]).then_inc(s["mb_out"], 16)
            sp.wait_ge(s["mb_out"], 16)
            for P in range(3):
                mask_row(Unit(None, P))
            max_row(Unit(None, 0))
            unit(Unit(None, 0))
            with sp.Fori(0, B - 1) as b:
                for i in range(1, HKV + 1):
                    unit(Unit(b, i))
            for i in range(UNITS - 3, UNITS):
                unit(Unit(None, i))
            sp.wait_ge(s["bias_done"], NEAR * UNITS)
            sp.wait_ge(s["pv_ps"], KT * UNITS)
            sp.dma_start(b2_sb[:, :, :], b2.partition_broadcast(128)).then_inc(s["ffw_in"], 16)
            sp.dma_start(W1.rearrange("p (e h) -> p e h", e=NE), w1.rearrange("e d h -> d e h")).then_inc(s["ffw_in"], 16)
            sp.dma_start(W2, w2).then_inc(s["ffw_in"], 16)
            with sp.Fori(0, TT // TG) as t:
                sp.wait_ge(s["f_y"], t * (NE * TG) + NE * TG)
                sp.dma_start(out[ds(t * (TG // QT), TG // QT), :, :].rearrange("b (q p) d -> p (b q) d", p=128),
                             X[:, ds(t * TG, TG), :]).then_inc(s["out_done"], 16)
            sp.wait_ge(s["out_done"], 16 * (TT // TG))

        @block.gpsimd
        def _(pool):
            pool.memset(ctx_sb[:, S2:KP], 0.0).then_inc(s["init_pool"], 1)
            for n, (dst, value) in enumerate(((K1[D:128, :, :], 0.0), (Q1[D:128, :, :], 0.0), (onerow, 1.0),
                                              (bigrow, BIG_Q))):
                pool.wait_ge(s["init_pool"], n + 1)
                pool.memset(dst, value).then_inc(s["init_pool"], 1)

            def add(u, t):
                if t == 0:
                    return
                n = KT * u.g + t
                acc = esum[:, u.g % 2, :]
                pool.wait_ge(s["e_up"], u.count(KT, t + 1))
                if t == 1:
                    if u.is_at_least(2):
                        pool.wait_ge(s["den_ps"], u.count(1, -1))
                    pool.tensor_tensor(acc, E[:, (n - 1) % ERING, :], E[:, n % ERING, :], ALU.add)\
                        .then_inc(s["sum_up"], 1)
                else:
                    pool.wait_ge(s["sum_up"], u.count(KT - 1, t - 1))
                    pool.tensor_tensor(acc, acc, E[:, n % ERING, :], ALU.add).then_inc(s["sum_up"], 1)

            def unit(u):
                for t in range(KT):
                    add(u, t)

            unit(Unit(None, 0))
            with pool.Fori(0, B - 1) as b:
                for i in range(1, HKV + 1):
                    unit(Unit(b, i))
            for i in range(UNITS - 3, UNITS):
                unit(Unit(None, i))

        @block.scalar
        def _(act):
            act.wait_ge(s["var_up"], 1)
            act.activation(std[:, :], std[:, :], ACT.Sqrt).then_inc(s["std_up"], 1)
            act.wait_ge(s["const_in"], 16 * N_CONST)
            act.activation(tg_[:, :], gx[:, :], ACT.Tanh).then_inc(s["tanh_up"], 1)

            def kv(P, r):
                t0, n = KV_ROUNDS[r]
                act.wait_ge(s["k_rope"], P.count(16, 4 * r + 3))
                if r == 0 and not P.is_at_least(1):
                    act.wait_ge(s["rows_in"], 16 * 2 * HKV)
                if r == 0 and P.is_at_least(HKV):
                    act.wait_ge(s["pv_ps"], P.count(KT, -3 * KT))
                act.activation(V[:, P.g, t0:t0 + n, :], mp_kv[:, 0:n, D:2 * D], ACT.Copy).then_inc(s["v_sb"], 1)

            def k_high(P):
                act.wait_ge(s["k_rope"], P.count(16, 16))
                if P.is_at_least(1):
                    act.wait_ge(s["kt_ps"], P.count(2))
                act.activation(khl[:, :, 0:D], kr[:, :, :], ACT.Copy).then_inc(s["kh_up"], 1)

            def q_high(P):
                act.wait_ge(s["q_rope"], P.count(4, 4))
                if P.is_at_least(1):
                    act.wait_ge(s["qt_ps"], P.count(1))
                act.activation(qhl[:, :, :, D:2 * D], qr[:, :, :, :], ACT.Copy).then_inc(s["qh_up"], 1)

            def k_out(P, r):
                t0, n = KTR[r]
                act.wait_ge(s["kt_ps"], P.count(2, r + 1))
                if r == 0 and P.is_at_least(HKV):
                    act.wait_ge(s["st_ps"], P.count(KT, -3 * KT))
                act.activation(K1[0:D, P.g, t0 * 128:(t0 + n) * 128], mp16[0:D, 0:n * 128], ACT.Copy)\
                   .then_inc(s["k1_sb"], 1)
                act.activation(K2[:, P.g, t0 * 128:(t0 + n) * 128], mp16[:, 0:n * 128], ACT.Copy)\
                   .then_inc(s["k2_sb"], 1)

            def q_out(P):
                act.wait_ge(s["qt_ps"], P.count(1, 1))
                act.activation(Q1[0:D, P.g, :], mp16[D:2 * D, 0:UC], ACT.Copy).then_inc(s["q1_sb"], 1)
                act.activation(Q2[:, P.g, :], mp16[:, 0:UC], ACT.Copy).then_inc(s["q2_sb"], 1)

            def exp(u, t):
                n = KT * u.g + t
                if t < NEAR:
                    act.wait_ge(s["bias_done"], u.count(NEAR, t + 1))
                else:
                    act.wait_ge(s["st_ps"], u.count(KT, t + 1))
                if not (u.reg is None and u.c == 0 and t < ERING):
                    act.wait_ge(s["pv_ps"], u.count(KT, t - ERING + 1))
                    k = t - ERING
                    off = max(k, 1) if k >= 0 else k + KT - (KT - 1)
                    act.wait_ge(s["sum_up"], u.count(KT - 1, off))
                act.activation(E[:, n % ERING, :], stp[n % 2][:, :], ACT.Exp).then_inc(s["e_up"], 1)

            def o_out(u):
                act.wait_ge(s["pv_ps"], u.count(KT, KT))
                if u.is_at_least(1):
                    act.wait_ge(s["wo_ps"], u.count(1))
                act.activation(oraw[:, :], op[:, :], ACT.Copy).then_inc(s["o_sb"], 1)

            def unit(u):
                P = u.at(3)
                prep = u.is_at_most(UNITS - 4)
                for t in range(KT):
                    if t == 0 and u.is_at_least(1):
                        o_out(u.at(-1))
                    if t + 1 < KT:
                        exp(u, t + 1)
                    elif u.is_at_most(UNITS - 2):
                        exp(u.at(1), 0)
                    if prep:
                        if 4 <= t < 8:
                            kv(P, t - 4)
                        if t == 8:
                            k_high(P)
                        if t == 9:
                            q_high(P)
                            k_out(P, 0)
                        if t == 10:
                            k_out(P, 1)
                        if t == 11:
                            q_out(P)

            for P in range(3):
                P = Unit(None, P)
                for r in range(4):
                    kv(P, r)
                k_high(P)
                q_high(P)
                k_out(P, 0)
                k_out(P, 1)
                q_out(P)
            exp(Unit(None, 0), 0)
            unit(Unit(None, 0))
            with act.Fori(0, B - 1) as b:
                for i in range(1, HKV + 1):
                    unit(Unit(b, i))
            for i in range(UNITS - 3, UNITS):
                unit(Unit(None, i))
            o_out(Unit(None, UNITS - 1))

            act.wait_ge(s["f_stats"], 2 * TT + 1)
            act.activation(std[:, :], std[:, :], ACT.Sqrt).then_inc(s["f_std"], 1)
            act.nop().then_inc(s["f_xT_act"], 1)
            with act.Fori(0, TT // TG) as t:
                act.wait_ge(s["f_xt_ps"], t + 2)
                act.activation(xTs, stp[0][:, 0:512], ACT.Copy).then_inc(s["f_xT_act"], 1)
            act.wait_ge(s["f_sub"], 2)
            act.activation(pr[:, :, :], lg[:, :, :], ACT.Exp).then_inc(s["f_exp"], 1)
            act.nop().then_inc(s["f_gelu"], HC)
            with act.Fori(0, TT // TG) as t:
                for e in range(NE):
                    for c in range(HC):
                        k = e * HC + c
                        act.wait_ge(s["f_h_ps"], t * (NE * HC) + k + 1)
                        if c == 0:
                            act.wait_ge(s["f_o_ps"], t * NE + e + 1)
                        act.activation(hid[:, ((e % 2) * HC + c) * 512:((e % 2) * HC + c + 1) * 512],
                                       stp[k // 2 % 2][:, 512 * (k % 2):512 * (k % 2) + 512], ACT.Gelu,
                                       bias=b1_sb[:, k:k + 1]).then_inc(s["f_gelu"], 1)

        @block.tensor
        def _(pe):
            pe.wait_ge(s["const_in"], 16 * N_CONST)
            pe.wait_ge(s["ident_up"], 1)
            pe.wait_ge(s["init_dve"], 1)
            pe.wait_ge(s["mask_f_up"], 2)
            for t in range(KT):
                last = pe.transpose(mp[:, t * B:(t + 1) * B], mask_f[:, t * 128:(t + 1) * 128], ident[0:B, 0:B])
            last.then_inc(s["mask_ps"], 1)
            pe.wait_ge(s["mask_sb"], 1)
            pe.wait_ge(s["any_up"], 2)
            pe.matmul(mp[:, 0:B], ones[0:B, :], diag16[:, :], start=True, stop=True).then_inc(s["any_ps"], 1)
            pe.wait_ge(s["any_sb"], 1)

            def xt(b_sem):
                pe.wait_ge(s["xn_up"], b_sem)
                for q in range(QT):
                    last = pe.transpose(mp[:, q * 128:(q + 1) * 128], xn[:, q, :], ident[:, :])
                last.then_inc(s["xt_ps"], 1)

            def kv(P, r):
                t0, n = KV_ROUNDS[r]
                if r:
                    pe.wait_ge(s["v_sb"], P.count(4, r))
                    pe.wait_ge(s["k_rope"], P.count(16, 4 * r - 1))
                else:
                    pe.wait_ge(s["ctx_in"], P.batch(16, 16))
                for j in range(n):
                    last = pe.matmul(mp_kv[:, j, :], ctx_sb[:, (t0 + j) * 128:(t0 + j + 1) * 128],
                                     wkv_sb[:, P.g, :], start=True, stop=True)
                last.then_inc(s["kv_ps"], 1)

            def q_proj(P):
                pe.wait_ge(s["v_sb"], P.count(4, 4))
                pe.wait_ge(s["k_rope"], P.count(16, 15))
                pe.wait_ge(s["xnT_sb"], P.batch(1, 1))
                for q in range(QT):
                    last = pe.matmul(mp[:, q * 256:(q + 1) * 256], xnT[:, q * 128:(q + 1) * 128],
                                     wq_sb[:, P.g * G * D:(P.g + 1) * G * D], start=True, stop=True)
                last.then_inc(s["q_ps"], 1)

            def k_turn(P, r):
                t0, n = KTR[r]
                if r:
                    pe.wait_ge(s["k2_sb"], P.count(2, 1))
                    pe.wait_ge(s["k1_sb"], P.count(2, 1))
                else:
                    pe.wait_ge(s["q_rope"], P.count(4, 3))
                    pe.wait_ge(s["kh_up"], P.count(1, 1))
                    pe.wait_ge(s["kl_up"], P.count(1, 1))
                for j in range(n):
                    last = pe.transpose(mp16[:, j * 128:(j + 1) * 128], khl[:, t0 + j, :], ident16[:, :])
                last.then_inc(s["kt_ps"], 1)

            def q_turn(P):
                pe.wait_ge(s["k2_sb"], P.count(2, 2))
                pe.wait_ge(s["k1_sb"], P.count(2, 2))
                pe.wait_ge(s["qh_up"], P.count(1, 1))
                pe.wait_ge(s["ql_up"], P.count(1, 1))
                for j in range(G):
                    for q in range(QT):
                        c = (j * QT + q) * 128
                        last = pe.transpose(mp16[:, c:c + 128], qhl[:, q, j, :], ident16[:, :])
                last.then_inc(s["qt_ps"], 1)

            def turned(n):
                pe.wait_ge(s["q1_sb"], n)
                pe.wait_ge(s["q2_sb"], n)

            def chunk(A, i):
                if i == 0:
                    turned(A.count(1, 1))
                    pe.wait_ge(s["k1_sb"], A.count(2, 2))
                    pe.wait_ge(mbrow_in[A.g], A.batch(16, 16))
                    if A.is_at_least(HKV):
                        pe.wait_ge(s["zrow"], A.count(1, 1 - HKV))
                    else:
                        pe.wait_ge(s["rows_in"], 16 * 2 * HKV)
                if not (A.reg is None and A.c == 0 and i < 2):
                    pe.wait_ge(s["pa_max"], A.count(PA, i - 1))
                hq, c = divmod(i, NCH)
                k0, n, _ = CHUNKS[c]
                pe.matmul(pap[i % 2][:, 0:n], Q1[:, A.g, hq * 128:(hq + 1) * 128], K1[:, A.g, k0:k0 + n],
                          start=True, stop=True).then_inc(s["pa_ps"], 1)

            def m_turn(A):
                pe.wait_ge(s["m16_up"], A.count(1, 1))
                pe.transpose(mp16[0:G * QT, 0:128], m16[:, :], ident16[:, :]).then_inc(s["mt_ps"], 1)

            def scores(u, t):
                n = KT * u.g + t
                if t == 0:
                    pe.wait_ge(s["mrow_in"], u.count(16, 16))
                    pe.wait_ge(s["k2_sb"], u.count(2, 2))
                if not (u.reg is None and u.c == 0 and t < 2):
                    pe.wait_ge(s["e_up"], u.count(KT, t - 1))
                for hf in range(2):
                    cols = slice(hf * 512, hf * 512 + 512)
                    pe.matmul(stp[n % 2][:, cols], K1[:, u.g, t * 128:(t + 1) * 128], Q1[:, u.g, cols],
                              start=True, stop=False)
                    last = pe.matmul(stp[n % 2][:, cols], K2[:, u.g, t * 128:(t + 1) * 128], Q2[:, u.g, cols],
                                     start=False, stop=True)
                last.then_inc(s["st_ps"], 1)

            def pv(u, t):
                n = KT * u.g + t
                pe.wait_ge(s["e_up"], u.count(KT, t + 1))
                if t == 0 and u.is_at_least(1):
                    pe.wait_ge(s["o_sb"], u.count(1))
                for hf in range(2):
                    last = pe.matmul(op[hf * 64:hf * 64 + 64, :], V[:, u.g, t, :],
                                     E[:, n % ERING, hf * 512:hf * 512 + 512], start=(t == 0), stop=(t == KT - 1))
                last.then_inc(s["pv_ps"], 1)

            def den(u):
                pe.wait_ge(s["sum_up"], u.count(KT - 1, KT - 1))
                for hf in range(2):
                    last = pe.matmul(mp[hf * 64:hf * 64 + 64, :], ones[:, 0:64],
                                     esum[:, u.g % 2, hf * 512:hf * 512 + 512], start=True, stop=True)
                last.then_inc(s["den_ps"], 1)

            def out_proj(u):
                pe.wait_ge(s["on_up"], u.count(1, 1))
                for q in range(QT):
                    for hh in range(2):
                        last = pe.matmul(mp[:, q * 128:(q + 1) * 128],
                                         onorm[:, hh * 256 + q * 128:hh * 256 + (q + 1) * 128],
                                         wo_sb[:, u.g * 2 + hh, :], start=(hh == 0), stop=(hh == 1))
                last.then_inc(s["wo_ps"], 1)

            def unit(u):
                P, A = u.at(3), u.at(2)
                prep, passa = u.is_at_most(UNITS - 4), u.is_at_most(UNITS - 3)
                for t in range(KT):
                    if t + 1 < KT:
                        scores(u, t + 1)
                    elif u.is_at_most(UNITS - 2):
                        scores(u.at(1), 0)
                    if passa:
                        for i in range(PA_FROM[t], PA_FROM[t + 1]):
                            chunk(A, i)
                    if t == 0 and u.g == 1 and prep:
                        turned(P.count(1))
                        xt(u.batch(1, 2))
                    if t == 1 and u.is_at_least(1):
                        if u.is_at_most(UNITS - 3):
                            turned(P.count(1))
                        if u.g == 1 and prep:
                            pe.wait_ge(s["xnT_sb"], u.batch(1, 2))
                        if u.is_at_least(2):
                            pe.wait_ge(s["y_up"], u.count(1, -1))
                        den(u.at(-1))
                    if t == 2 and u.is_at_most(UNITS - 2):
                        if u.is_at_least(1):
                            pe.wait_ge(s["rden_up"], u.count(1))
                        else:
                            turned(3)
                        m_turn(u.at(1))
                    if t == 3 and u.is_at_least(1):
                        if u.is_at_most(UNITS - 2):
                            pe.wait_ge(s["mT_sb"], u.count(1, 2))
                        else:
                            pe.wait_ge(s["rden_up"], u.count(1))
                        out_proj(u.at(-1))
                    if prep:
                        if t == 4:
                            if u.is_at_least(1):
                                pe.wait_ge(s["y_up"], u.count(1))
                            else:
                                pe.wait_ge(s["mT_sb"], 2)
                        if 4 <= t < 8:
                            kv(P, t - 4)
                        if t == 8:
                            q_proj(P)
                        if t == 9:
                            k_turn(P, 0)
                        if t == 10:
                            k_turn(P, 1)
                        if t == 11:
                            q_turn(P)
                    pv(u, t)

            xt(1)
            pe.wait_ge(s["xnT_sb"], 1)
            for P in range(3):
                P = Unit(None, P)
                if P.c:
                    turned(P.c)
                for r in range(4):
                    kv(P, r)
                q_proj(P)
                k_turn(P, 0)
                k_turn(P, 1)
                q_turn(P)
            for A in range(2):
                for i in range(PA):
                    chunk(Unit(None, A), i)
            turned(3)
            m_turn(Unit(None, 0))
            pe.wait_ge(s["mT_sb"], 1)
            scores(Unit(None, 0), 0)
            unit(Unit(None, 0))
            with pe.Fori(0, B - 1) as b:
                for i in range(1, HKV + 1):
                    unit(Unit(b, i))
            for i in range(UNITS - 3, UNITS):
                unit(Unit(None, i))
            last_u = Unit(None, UNITS - 1)
            pe.wait_ge(s["y_up"], UNITS - 1)
            den(last_u)
            pe.wait_ge(s["rden_up"], UNITS)
            out_proj(last_u)

            pe.nop().then_inc(s["f_xt_ps"], 1)
            with pe.Fori(0, TT // TG) as t:
                pe.wait_ge(s["f_xn"], t + 1)
                pe.wait_ge(s["f_xT_dve"], t + 1)
                pe.wait_ge(s["f_xT_act"], t + 1)
                for j in range(TG):
                    last = pe.transpose(stp[0][:, j * 128:(j + 1) * 128], xn[:, j, :], ident[:, :])
                last.then_inc(s["f_xt_ps"], 1)
                pe.wait_ge(s["f_xT_act"], t + 2)
                pe.wait_ge(s["f_lg"], t + 1)
                for j in range(TG):
                    last = pe.matmul(mp[:, j * NE:(j + 1) * NE], xTs[:, j * 128:(j + 1) * 128], gate_sb[:, :],
                                     start=True, stop=True)
                last.then_inc(s["f_lg_ps"], 1)

            pe.wait_ge(s["ffw_in"], 48)
            pe.wait_ge(s["f_xT_dve"], TT // TG + 1)

            def up(t, e):
                for c in range(HC):
                    k = e * HC + c
                    pe.wait_ge(s["f_gelu"], t * (NE * HC) + k + 1)
                    pe.matmul(stp[k // 2 % 2][:, 512 * (k % 2):512 * (k % 2) + 512], W1[:, k * 128:(k + 1) * 128],
                              XT2[:, ds(t * 512, 512)], start=True, stop=True).then_inc(s["f_h_ps"], 1)

            def down(t, e):
                pe.wait_ge(s["f_gelu"], t * (NE * HC) + (e + 2) * HC)
                pe.wait_ge(s["f_ob"], t * NE + e + 1)
                for j in range(TG):
                    for c in range(HC):
                        a = ((e % 2) * HC + c) * 512 + j * 128
                        last = pe.matmul(pap[e % 2][:, j * 128:(j + 1) * 128], hid[:, a:a + 128],
                                         W2[:, (e * HC + c) * 128:(e * HC + c + 1) * 128],
                                         start=(c == 0), stop=(c == HC - 1))
                last.then_inc(s["f_o_ps"], 1)

            pe.nop().then_inc(s["f_o_ps"], 2)
            with pe.Fori(0, TT // TG) as t:
                up(t, 0)
                for e in range(NE):
                    if e + 1 < NE:
                        up(t, e + 1)
                    down(t, e)

        @block.vector
        def _(dve):
            dve.memset(ones[:, :], 1.0).then_inc(s["init_dve"], 1)
            dve.memset(mask_f, 0.0).then_inc(s["mask_f_up"], 1)
            dve.memset(mb16[:, S2:KP], BIG_K).then_inc(s["mb_up"], 1)
            dve.wait_ge(s["x_in"], 32)
            dve.wait_ge(s["mask_f_up"], 1)
            dve.tensor_copy(mask_f[:, 0:S2], mask_u8[:, :]).then_inc(s["mask_f_up"], 1)
            for j in range(TT):
                dve.bn_stats(stats[:, j, :], X[:, j, :]).then_inc(s["f_stats"], 1)
            dve.wait_ge(s["mask_f_up"], 2)
            dve.tensor_reduce(any16[:, :], mask_f, AX.X, ALU.max).then_inc(s["any_up"], 1)
            dve.tensor_scalar(mask_t, mask_f, -1.0, -BIG_K, ALU.add, ALU.mult).then_inc(s["mb_up"], 1)
            for j in range(TT):
                dve.wait_ge(s["f_stats"], j + 1)
                dve.bn_aggr(mv[:, j, :], stats[:, j, :]).then_inc(s["rstd_up"], 1)
            dve.wait_ge(s["rstd_up"], TT)
            dve.tensor_scalar(std[:, :], mv[:, :, 1], 1e-5, None, ALU.add).then_inc(s["var_up"], 1)
            dve.wait_ge(s["const_in"], 16 * N_CONST)
            dve.tensor_copy(ident16[:, :], ident[:, :]).then_inc(s["ident_up"], 1)
            dve.wait_ge(s["any_up"], 1)
            dve.tensor_scalar(diag16[:, :], ident[0:B, 0:B], any16[:, 0:1], None, ALU.mult).then_inc(s["any_up"], 1)
            dve.wait_ge(s["mb_up"], 2)
            dve.tensor_scalar(mb16[:, 0:S2], mask_t[:, 0:S2], any16[:, 0:1], None, ALU.mult).then_inc(s["mb_up"], 1)
            dve.wait_ge(s["mask_ps"], 1)
            dve.tensor_copy(maskT[:, :, :].rearrange("p b t -> p t b"),
                            mp[:, 0:KT * B].rearrange("p (t b) -> p t b", t=KT)).then_inc(s["mask_sb"], 1)
            dve.wait_ge(s["any_ps"], 1)
            dve.tensor_copy(anyb[:, :], mp[:, 0:B]).then_inc(s["any_sb"], 1)
            dve.wait_ge(s["std_up"], 1)
            dve.reciprocal(rstd[:, :], std[:, :]).then_inc(s["rstd_up"], 1)
            dve.wait_ge(s["rstd_up"], TT + 1)
            dve.wait_ge(s["mask_sb"], 1)

            def normalise(bt, n, done):
                if n is not None:
                    dve.wait_ge(s["xt_ps"], n)
                for q in range(QT):
                    last = dve.tensor_scalar(xn[:, q, :], X[:, ds(bt * QT + q, 1), :].rearrange("p o d -> p (o d)"),
                                             mv[:, ds(bt * QT + q, 1), 0:1].rearrange("p o d -> p (o d)"),
                                             rstd[:, ds(bt * QT + q, 1)], ALU.subtract, ALU.mult)
                last.then_inc(s["xn_up"], 1)

            def mask_rope(bt, n):
                if n is not None:
                    dve.wait_ge(s["k_rope"], n)
                m = maskT[:, ds(bt, 1), :].rearrange("p o t -> p (o t)").unsqueeze(2).broadcast_to([128, KT, 2 * D])
                dve.tensor_tensor(rkm[:, :, :, :].rearrange("p t a d -> p t (a d)"),
                                  rk[:, :, :, :].rearrange("p t a d -> p t (a d)"), m, ALU.mult)\
                   .then_inc(s["rkm_up"], 1)

            def xt_out(n):
                dve.wait_ge(s["xt_ps"], n)
                dve.tensor_copy(xnT[:, :], mp[:, 0:M]).then_inc(s["xnT_sb"], 1)

            def kv(P, r):
                t0, n = KV_ROUNDS[r]
                if r == 0:
                    dve.wait_ge(s["rkm_up"], P.batch(1, 1))
                    if P.is_at_least(1):
                        dve.wait_ge(s["kh_up"], P.count(1))
                        dve.wait_ge(s["kl_up"], P.count(1))
                if not (P.reg is None and P.c == 0 and r == 0):
                    dve.wait_ge(s["k_rope"], P.count(16, 4 * r))
                dve.wait_ge(s["kv_ps"], P.count(4, r + 1))
                h = D // 2
                dve.tensor_tensor(kt1[:, 0:n, :], mp_kv[:, 0:n, 0:D], rkm[:, t0:t0 + n, 0, :], ALU.mult)\
                   .then_inc(s["k_rope"], 1)
                dve.tensor_tensor(kt2[:, 0:n, 0:h], mp_kv[:, 0:n, h:D], rkm[:, t0:t0 + n, 1, 0:h], ALU.mult)\
                   .then_inc(s["k_rope"], 1)
                dve.tensor_tensor(kt2[:, 0:n, h:D], mp_kv[:, 0:n, 0:h], rkm[:, t0:t0 + n, 1, h:D], ALU.mult)\
                   .then_inc(s["k_rope"], 1)
                dve.wait_ge(s["k_rope"], P.count(16, 4 * r + 3))
                dve.tensor_tensor(kr[:, t0:t0 + n, :], kt1[:, 0:n, :], kt2[:, 0:n, :], ALU.add)\
                   .then_inc(s["k_rope"], 1)

            def k_low(P):
                dve.wait_ge(s["kh_up"], P.count(1, 1))
                dve.tensor_tensor(khl[:, :, D:2 * D], kr[:, :, :], khl[:, :, 0:D], ALU.subtract)\
                   .then_inc(s["kl_up"], 1)

            def q_rope(P):
                h = D // 2
                dve.wait_ge(s["q_ps"], P.count(1, 1))
                if P.is_at_least(1):
                    dve.wait_ge(s["q_rope"], P.count(4))
                    dve.wait_ge(s["qh_up"], P.count(1))
                    dve.wait_ge(s["ql_up"], P.count(1))
                m = mp[:, :].rearrange("p (q j d) -> p q j d", q=QT, j=G)
                cos = rq[:, :, 0:1, :].broadcast_to([128, QT, G, D])
                dve.tensor_tensor(qt1[:, :, :, :], m, cos, ALU.mult).then_inc(s["q_rope"], 1)
                dve.tensor_tensor(qt2[:, :, :, 0:h], m[:, :, :, h:D],
                                  rq[:, :, 1:2, 0:h].broadcast_to([128, QT, G, h]), ALU.mult).then_inc(s["q_rope"], 1)
                dve.tensor_tensor(qt2[:, :, :, h:D], m[:, :, :, 0:h],
                                  rq[:, :, 1:2, h:D].broadcast_to([128, QT, G, h]), ALU.mult).then_inc(s["q_rope"], 1)
                dve.wait_ge(s["q_rope"], P.count(4, 3))
                dve.tensor_tensor(qr[:, :, :, :], qt1[:, :, :, :], qt2[:, :, :, :], ALU.add).then_inc(s["q_rope"], 1)

            def q_low(P):
                dve.wait_ge(s["qh_up"], P.count(1, 1))
                dve.tensor_tensor(qhl[:, :, :, 0:D], qr[:, :, :, :], qhl[:, :, :, D:2 * D], ALU.subtract)\
                   .then_inc(s["ql_up"], 1)

            def chunk(A, i):
                hq, c = divmod(i, NCH)
                j, q = divmod(hq, QT)
                k0, n, with_bias = CHUNKS[c]
                if i == 0 and A.is_at_least(1):
                    dve.wait_ge(s["pm_red"], A.count(1))
                dve.wait_ge(s["pa_ps"], A.count(PA, i + 1))
                if with_bias:
                    a = 128 * q + k0
                    if not (A.reg is None and A.c == 0 and i < 2):
                        dve.wait_ge(s["pa_max"], A.count(PA, i - 1))
                    dve.sem_inc(s["pa_seen"], 1)
                    dve.tensor_tensor_reduce(junk[:, i % 2, :], pap[i % 2][:, 0:n], WB[:, A.g * G + j, a:a + n], 1.0,
                                             -3.0e38, ALU.add, ALU.max, pm[:, hq, c:c + 1]).then_inc(s["pa_max"], 1)
                else:
                    dve.tensor_reduce(pm[:, hq, c:c + 1], pap[i % 2][:, 0:n], AX.X, ALU.max)\
                       .then_inc(s["pa_max"], 1)

            def zero_row(P):
                dve.wait_ge(s["st_ps"], P.count(KT, -3 * KT))
                dve.memset(Q1[D:D + 1, P.g, :], 0.0).then_inc(s["zrow"], 1)

            def maxima(A):
                dve.wait_ge(s["pa_max"], A.count(PA, PA))
                if A.is_at_least(1):
                    dve.wait_ge(s["m16_up"], A.count(1))
                dve.tensor_reduce(mred[:, :], pm[:, :, :], AX.X, ALU.max).then_inc(s["pm_red"], 1)
                dve.wait_ge(s["pm_red"], A.count(1, 1))
                if A.is_at_least(1):
                    dve.wait_ge(s["mt_ps"], A.count(1))
                dve.tensor_scalar(m16[:, :], mred[:, :], anyb[:, ds(A.batch(), 1)], -1.0, ALU.mult, ALU.mult)\
                   .then_inc(s["m16_up"], 1)

            def m_out(A):
                dve.wait_ge(s["mt_ps"], A.count(1, 1))
                if A.is_at_least(1):
                    dve.wait_ge(s["mrow_in"], A.count(16))
                dve.tensor_copy(mT[:, :], mp16[0:G * QT, 0:128]).then_inc(s["mT_sb"], 1)

            def bias(u, t):
                n = KT * u.g + t
                dve.wait_ge(s["st_ps"], u.count(KT, t + 1))
                p3 = stp[n % 2][:, :].rearrange("p (j i) -> p j i", j=G)
                dve.scalar_tensor_tensor(p3, WB[:, u.g * G:(u.g + 1) * G, t * 128:t * 128 + M],
                                         maskT[:, ds(u.batch(), 1), t:t + 1].rearrange("p o t -> p (o t)"), p3,
                                         ALU.mult, ALU.add).then_inc(s["bias_done"], 1)

            def den(u):
                dve.wait_ge(s["den_ps"], u.count(1, 1))
                if u.is_at_least(1):
                    dve.wait_ge(s["on_up"], u.count(1))
                dve.reciprocal(rden[:, :], mp[:, :]).then_inc(s["rden_up"], 1)
                dve.wait_ge(s["rden_up"], u.count(1, 1))
                dve.wait_ge(s["o_sb"], u.count(1, 1))
                dve.tensor_tensor(onorm[:, :], oraw[:, :], rden[:, :], ALU.mult).then_inc(s["on_up"], 1)

            def residual(u):
                dve.wait_ge(s["wo_ps"], u.count(1, 1))
                if u.is_at_least(1):
                    dve.wait_ge(s["y_up"], u.count(1))
                xs = X[:, ds(u.batch(QT), QT), :].rearrange("p q d -> p (q d)")
                dve.scalar_tensor_tensor(xs, mp[:, 0:M], tg_[:, 0:1], xs, ALU.mult, ALU.add).then_inc(s["y_up"], 1)

            def unit(u):
                P, A = u.at(3), u.at(2)
                prep, passa = u.is_at_most(UNITS - 4), u.is_at_most(UNITS - 3)
                for t in range(KT):
                    if t + 1 < NEAR:
                        bias(u, t + 1)
                    elif t == KT - 1 and u.is_at_most(UNITS - 2):
                        bias(u.at(1), 0)
                    if t == 0 and u.g == 1 and prep:
                        normalise(u.batch(1, 1), u.batch(1, 1), None)
                        mask_rope(u.batch(1, 1), u.count(16, 48))
                    if passa:
                        for i in range(PA_FROM[t], PA_FROM[t + 1]):
                            chunk(A, i)
                    if t == 0 and u.g == 1 and prep:
                        xt_out(u.batch(1, 2))
                    if t == 1 and u.is_at_least(1):
                        den(u.at(-1))
                    if t == 2 and u.is_at_most(UNITS - 2):
                        m_out(u.at(1))
                    if t == 3 and u.is_at_least(1):
                        residual(u.at(-1))
                    if prep:
                        if 4 <= t < 8:
                            kv(P, t - 4)
                        if t == 8:
                            k_low(P)
                            q_rope(P)
                        if t == 9:
                            q_low(P)
                        if t == 11 and P.is_at_least(HKV):
                            zero_row(P)
                    if t == 12 and passa:
                        maxima(A)

            normalise(0, None, None)
            mask_rope(0, None)
            dve.wait_ge(s["bias_in"], 16)
            for h in range(H):
                dve.tensor_scalar(WB[:, h, :], WB[:, h, :], far[:, h:h + 1], None, ALU.subtract)\
                   .then_inc(s["bias_up"], 1)
            dve.wait_ge(s["bias_up"], H)
            dve.wait_ge(s["any_sb"], 1)
            dve.wait_ge(s["tanh_up"], 1)
            xt_out(1)
            for P in range(3):
                P = Unit(None, P)
                for r in range(4):
                    kv(P, r)
                k_low(P)
                q_rope(P)
                q_low(P)
            for A in range(2):
                for i in range(PA):
                    chunk(Unit(None, A), i)
                if A == 1:
                    m_out(Unit(None, 0))
                maxima(Unit(None, A))
            bias(Unit(None, 0), 0)
            unit(Unit(None, 0))
            with dve.Fori(0, B - 1) as b:
                for i in range(1, HKV + 1):
                    unit(Unit(b, i))
            for i in range(UNITS - 3, UNITS):
                unit(Unit(None, i))
            last_u = Unit(None, UNITS - 1)
            den(last_u)
            residual(last_u)

            dve.wait_ge(s["y_up"], UNITS)
            for j in range(TT):
                dve.bn_stats(stats[:, j, :], X[:, j, :]).then_inc(s["f_stats"], 1)
            for j in range(TT):
                dve.wait_ge(s["f_stats"], TT + j + 1)
                dve.bn_aggr(mv[:, j, :], stats[:, j, :]).then_inc(s["f_rstd"], 1)
            dve.wait_ge(s["f_rstd"], TT)
            dve.tensor_scalar(std[:, :], mv[:, :, 1], 1e-5, None, ALU.add).then_inc(s["f_stats"], 1)
            dve.wait_ge(s["f_std"], 1)
            dve.reciprocal(rstd[:, :], std[:, :]).then_inc(s["f_rstd"], 1)
            dve.memset(iota_r[:, :], 0.0).then_inc(s["f_rstd"], 1)
            dve.wait_ge(s["f_rstd"], TT + 2)
            for e in range(NE):
                dve.memset(iota_r[:, e:e + 1], float(NE - e)).then_inc(s["f_rstd"], 1)
            dve.nop().then_inc(s["f_xT_dve"], 1)
            dve.nop().then_inc(s["f_lg"], 1)
            with dve.Fori(0, TT // TG) as t:
                dve.wait_ge(s["f_xt_ps"], t + 1)
                for j in range(TG):
                    last = dve.tensor_scalar(xn[:, j, :], X[:, ds(t * TG + j, 1), :].rearrange("p o d -> p (o d)"),
                                             mv[:, ds(t * TG + j, 1), 0:1].rearrange("p o d -> p (o d)"),
                                             rstd[:, ds(t * TG + j, 1)], ALU.subtract, ALU.mult)
                last.then_inc(s["f_xn"], 1)
                dve.wait_ge(s["f_xt_ps"], t + 2)
                dve.wait_ge(s["f_xT_act"], t + 2)
                dve.tensor_copy(XT2[:, ds(t * 512, 512)], stp[0][:, 0:512]).then_inc(s["f_xT_dve"], 1)
                dve.wait_ge(s["f_lg_ps"], t + 1)
                dve.tensor_copy(lg[:, ds(t * TG, TG), :], mp[:, 0:TG * NE].rearrange("p (j e) -> p j e", e=NE))\
                   .then_inc(s["f_lg"], 1)

            def wide(v):
                return v[:, :].unsqueeze(2).broadcast_to([128, TT, NE])

            g_count = [0]

            def gate(ins):
                g_count[0] += 1
                ins.then_inc(s["f_gate"], 1)
                dve.wait_ge(s["f_gate"], g_count[0])

            dve.wait_ge(s["f_lg"], TT // TG + 1)
            dve.tensor_reduce(r1[:, :], lg[:, :, :], AX.X, ALU.max).then_inc(s["f_sub"], 1)
            dve.wait_ge(s["f_sub"], 1)
            dve.tensor_tensor(lg[:, :, :], lg[:, :, :], wide(r1), ALU.subtract).then_inc(s["f_sub"], 1)
            dve.wait_ge(s["f_exp"], 1)
            gate(dve.tensor_reduce(r1[:, :], pr[:, :, :], AX.X, ALU.add))
            gate(dve.reciprocal(r2[:, :], r1[:, :]))
            gate(dve.tensor_tensor(pr[:, :, :], pr[:, :, :], wide(r2), ALU.mult))
            order = iota_r[:, :].unsqueeze(1).broadcast_to([128, TT, NE])

            def first_max(src, sel, best):
                gate(dve.tensor_reduce(best[:, :], src, AX.X, ALU.max))
                gate(dve.tensor_tensor(sel, src, wide(best), ALU.is_equal))
                gate(dve.tensor_tensor(sel, sel, order, ALU.mult))
                gate(dve.tensor_reduce(r3[:, :], sel, AX.X, ALU.max))
                gate(dve.tensor_tensor(sel, order, wide(r3), ALU.is_equal))

            first_max(pr[:, :, :], wsel[:, :, :], r1)
            gate(dve.tensor_scalar(ga[:, :, :], wsel[:, :, :], -2.0, None, ALU.mult))
            gate(dve.tensor_tensor(ga[:, :, :], ga[:, :, :], pr[:, :, :], ALU.add))
            first_max(ga[:, :, :], gb[:, :, :], r2)
            gate(dve.tensor_tensor(wsel[:, :, :], wsel[:, :, :], gb[:, :, :], ALU.add))
            gate(dve.tensor_tensor(wsel[:, :, :], wsel[:, :, :], pr[:, :, :], ALU.mult))
            gate(dve.scalar_tensor_tensor(r3[:, :], r1[:, :], 1e-9, r2[:, :], ALU.add, ALU.add))
            gate(dve.reciprocal(r1[:, :], r3[:, :]))
            gate(dve.tensor_tensor(wsel[:, :, :], wsel[:, :, :], wide(r1), ALU.mult))
            gate(dve.tensor_scalar(wsel[:, :, :], wsel[:, :, :], tg_[:, 1:2], None, ALU.mult))

            dve.nop().then_inc(s["f_ob"], 1)
            dve.wait_ge(s["ffw_in"], 48)
            with dve.Fori(0, TT // TG) as t:
                for e in range(NE):
                    dve.wait_ge(s["f_o_ps"], t * NE + e + 3)
                    o = oe[:, (e % 2) * 512:(e % 2) * 512 + 512].rearrange("p (j d) -> p j d", j=TG)
                    b2e = b2_sb[:, e:e + 1, :].broadcast_to([128, TG, DM])
                    dve.tensor_tensor(o, pap[e % 2][:, :].rearrange("p (j d) -> p j d", j=TG), b2e, ALU.add)\
                       .then_inc(s["f_ob"], 1)
                    dve.wait_ge(s["f_ob"], t * NE + e + 2)
                    for j in range(TG):
                        xs = X[:, ds(t * TG + j, 1), :].rearrange("p o d -> p (o d)")
                        w = wsel[:, ds(t * TG + j, 1), e:e + 1].rearrange("p o d -> p (o d)")
                        if e:
                            dve.wait_ge(s["f_y"], t * (NE * TG) + (e - 1) * TG + j + 1)
                        dve.scalar_tensor_tensor(xs, o[:, j, :], w, xs, ALU.mult, ALU.add).then_inc(s["f_y"], 1)


def _constants():
    import numpy as np
    inv = np.float32(1) / (np.float64(10000.0) ** (np.arange(0, D, 2, dtype=np.float32) / np.float32(D)).astype(np.float64)).astype(np.float32)

    def table(pos, scale):
        f = np.repeat(np.outer(pos.astype(np.float32), inv), 2, axis=-1)
        cos, sin = np.cos(f), np.sin(f)
        sin[:, :D // 2] *= -1
        return (np.stack([cos, sin], 1) * np.float32(scale)).astype(np.float32)

    rk = table(np.arange(KP), 1.0).reshape(KT, 128, 2, D).transpose(1, 0, 2, 3)
    rq = table(M - 1 - np.arange(M), D ** -0.5).reshape(QT, 128, 2, D).transpose(1, 0, 2, 3)
    return np.ascontiguousarray(rk), np.ascontiguousarray(rq), np.eye(128, dtype=np.float32)


def kernel(x, ctx_1024, mask_BxS2_bf1, g_xattn, g_ffn, L0_xattn_Wq, L0_xattn_Wk, L0_xattn_Wv, L0_xattn_Wo,
           L0_xattn_rel_pos_bias, L0_ffn_gate_w, L0_ffn_w1, L0_ffn_b1, L0_ffn_w2, L0_ffn_b2):
    import numpy as np
    import concourse.bacc as bacc
    from concourse.bass_utils import run_bass_kernel_spmd

    a = np.asarray
    c = np.ascontiguousarray
    rk, rq, eye = _constants()
    wk, wv, wo, bias = a(L0_xattn_Wk), a(L0_xattn_Wv), a(L0_xattn_Wo), a(L0_xattn_rel_pos_bias)
    wkv = np.concatenate([wk.reshape(DM, HKV, D), wv.reshape(DM, HKV, D)], axis=2)
    wo2 = wo.reshape(HKV, 2, 2, D, DM).transpose(1, 3, 0, 2, 4).reshape(128, HKV * 2, DM)
    dist = np.minimum(np.abs(np.arange(WIN + 127) - (M - 1)), MAXREL - 1)
    arrays = {
        "x": c(a(x)[:, ::-1, :]), "ctxT": c(a(ctx_1024).transpose(0, 2, 1)), "mask": c(a(mask_BxS2_bf1)).view(np.uint8),
        "g_x": c(a(g_xattn)), "g_f": c(a(g_ffn)), "wq": c(a(L0_xattn_Wq)), "wkv": c(wkv), "wo2": c(wo2),
        "bias_f": c(bias[:, dist]), "bias_far": c(bias[:, MAXREL - 1]), "gateT": c(a(L0_ffn_gate_w).T),
        "w1": c(a(L0_ffn_w1)), "b1T": c(a(L0_ffn_b1).reshape(NE * HC, 128).T),
        "w2": c(a(L0_ffn_w2).reshape(NE * HC, 128, DM).transpose(1, 0, 2).reshape(128, NE * HC * DM)), "b2": c(a(L0_ffn_b2)),
        "rope_k": rk, "rope_q": rq, "ident": eye,
    }
    nc = bacc.Bacc("TRN2", target_bir_lowering=False, num_devices=1)
    args = [nc.dram_tensor(f"in_{k}", v.shape, mybir.dt.from_np(v.dtype), kind="ExternalInput").ap()
            for k, v in arrays.items()]
    out = nc.dram_tensor("out_0", [B, M, DM], mybir.dt.float32, kind="ExternalOutput").ap()
    flamingo_block(nc, *args, out)
    r = run_bass_kernel_spmd(nc, [{f"in_{k}": v for k, v in arrays.items()}], core_ids=[0])
    return r.results[0]["out_0"][:, ::-1, :]
```

```python
import concourse.bass as bass
from concourse import mybir
from contextlib import ExitStack

B, M, S2, DM = 16, 256, 1601, 128
H, HKV, D = 16, 4, 64
G = H // HKV
QT = M // 128
KT = (S2 + 127) // 128
KP = KT * 128
UNITS = B * HKV
UC = G * M
MAXREL = 384
NEAR = 5
WIN = (NEAR - 1) * 128 + M
SUM_UNIT = 2.0 ** -6
ERING = 4
NE, HID, TOPC = 8, 512, 2
HC = HID // 128
TT = B * QT
TG = 4
BIG_Q, BIG_K = 32768.0, -30528.0
CHUNKS = [(0, 320, True), (320, 320, True), (640, 481, False), (1121, 480, False)]
NCH = len(CHUNKS)
PA = G * QT * NCH
PA_STEPS = [2, 2, 2, 2, 3, 3, 3, 3, 1, 3, 3, 3, 2]
assert sum(PA_STEPS) == PA and len(PA_STEPS) == KT
PA_FROM = [sum(PA_STEPS[:t]) for t in range(KT + 1)]
KV_ROUNDS = [(r, min(4, KT - r)) for r in range(0, KT, 4)]
KTR = [(0, 7), (7, KT - 7)]


class Unit:

    def __init__(self, reg, c):
        self.reg, self.c = reg, c
        self.g = c % HKV

    def at(self, d):
        return Unit(self.reg, self.c + d)

    def count(self, k, off=0):
        c = k * self.c + off
        return c if self.reg is None else self.reg * (HKV * k) + c

    def batch(self, k=1, off=0):
        c = k * (self.c // HKV) + off
        return c if self.reg is None else self.reg * k + c

    def is_at_most(self, last):
        return self.reg is not None or self.c <= last

    def is_at_least(self, first):
        return self.reg is not None or self.c >= first


def flamingo_block(nc, x, ctxT, mask, g_x, g_f, wq, wkv, wo2, bias_f, bias_far, gateT, w1, b1T, w2, b2,
                   rope_k, rope_q, ident_in, zero_dram, out):
    F32, F16 = mybir.dt.float32, mybir.dt.float16
    ALU = mybir.AluOpType
    ACT = mybir.ActivationFunctionType
    AX = mybir.AxisListType
    ds = bass.ds
    mb_dram = nc.dram_tensor("mask_bias", [B, KP], F16, kind="Internal").ap()
    ctx = ExitStack()
    with ctx:
        def sb(name, shape, dt=F32):
            return ctx.enter_context(nc.sbuf_tensor(name, shape, dt))

        def ps(name, cols):
            return ctx.enter_context(nc.psum_tensor(name, [128, cols], F32))

        def sem(name):
            return ctx.enter_context(nc.semaphore(name))

        X = sb("X", [128, TT, DM])
        WB = sb("WB", [128, H, WIN])
        K1 = sb("K1", [128, HKV, KP], F16)
        K2 = sb("K2", [128, HKV, KP], F16)
        Q1 = sb("Q1", [128, HKV, UC], F16)
        Q2 = sb("Q2", [128, HKV, UC], F16)
        V = sb("V", [128, HKV, KT, D])
        E = sb("E", [128, ERING, UC])
        esum = sb("esum", [128, 2, UC])
        ctx_sb = sb("ctx_sb", [128, KP])
        kr = sb("kr", [128, KT, D])
        kt1 = sb("kt1", [128, 4, D])
        kt2 = sb("kt2", [128, 4, D])
        khl = sb("khl", [128, KT, 2 * D], F16)
        qr = sb("qr", [128, QT, G, D])
        qt1 = sb("qt1", [128, QT, G, D])
        qt2 = sb("qt2", [128, QT, G, D])
        qhl = sb("qhl", [128, QT, G, 2 * D], F16)
        oraw = sb("oraw", [128, 512])
        rden = sb("rden", [128, 512])
        wkv_sb = sb("wkv_sb", [128, HKV, 2 * D])
        wq_sb = sb("wq_sb", [128, H * D])
        wo_sb = sb("wo_sb", [128, HKV * 2, DM])
        rk = sb("rk", [128, KT, 2, D])
        rkm = sb("rkm", [128, KT, 2, D])
        rq = sb("rq", [128, QT, 2, D])
        xn = sb("xn", [128, TG, DM])
        xnT = sb("xnT", [128, M])
        ident = sb("ident", [128, 128])
        ident16 = sb("ident16", [128, 128], F16)
        ones = sb("ones", [128, 128])
        maskT = sb("maskT", [128, B, KT])
        anyb = sb("anyb", [128, B])
        any16 = sb("any16", [B, 1])
        diag16 = sb("diag16", [B, B])
        mb16 = sb("mb16", [B, KP], F16)
        far = sb("far", [128, H])
        pm = sb("pm", [128, G * QT, NCH])
        mred = sb("mred", [128, G * QT])
        m16 = sb("m16", [128, G * QT], F16)
        mT = sb("mT", [G * QT, 128], F16)
        junk = sb("junk", [128, 2, 320])
        stats = sb("stats", [128, TT, 6])
        mv = sb("mv", [128, TT, 2])
        std = sb("std", [128, TT])
        rstd = sb("rstd", [128, TT])
        nmr = sb("nmr", [128, TT])
        gx = sb("gx", [128, 2])
        tg_ = sb("tg_", [128, 2])
        gate_sb = sb("gate_sb", [128, NE])
        b1_sb = sb("b1_sb", [128, NE * HC])
        iota_r = sb("iota_r", [128, NE])
        r1 = sb("r1", [128, TT])
        r2 = sb("r2", [128, TT])
        r3 = sb("r3", [128, TT])
        onorm = oraw
        Vf = V[:, :, :, :].rearrange("p g t d -> p (g t d)")
        onerow = Vf[0:1, 0:KP // 2].bitcast(F16)
        bigrow = Vf[0:1, KP // 2:KP // 2 + UC // 2].bitcast(F16)
        mask_u8 = Vf[0:B, 1400:1400 + (S2 + 3) // 4].bitcast(mybir.dt.uint8)[:, 0:S2]
        lg, pr, ga, gb, wsel = (Vf[:, i * TT * NE:(i + 1) * TT * NE].rearrange("p (t e) -> p t e", e=NE)
                                for i in range(5))
        b2_sb = Vf[:, 2048:2048 + NE * DM].rearrange("p (e d) -> p e d", e=NE)
        mask_f = E[0:B, 0:2, :].rearrange("p a c -> p (a c)")[:, 0:KP]
        mask_t = E[0:B, 2:4, :].rearrange("p a c -> p (a c)")[:, 0:KP]
        WBf = WB[:, :, :].rearrange("p h w -> p (h w)")
        W1 = WBf[:, 0:NE * HID]
        W2 = WBf[:, NE * HID:2 * NE * HID]
        XT2 = WBf[:, 2 * NE * HID:2 * NE * HID + TT * 128]
        hid = E[:, :, :].rearrange("p r c -> p (r c)")
        oe = esum[:, :, :].rearrange("p a c -> p (a c)")
        xTs = ctx_sb[:, 0:512]

        stp = [ps(f"st{i}", UC) for i in range(2)]
        pap = [ps(f"pa{i}", 512) for i in range(2)]
        op = ps("op", 512)
        mp = ps("mp", 512)
        mp16 = mp[:, :].bitcast(F16)
        mp_kv = mp[:, :].rearrange("p (t c) -> p t c", t=4)

        names = """mb_out const_in x_in ctx_in mrow_in rows_in bias_in ffw_in out_done
            init_pool init_dve ident_up mask_f_up mask_ps mask_sb any_up any_ps any_sb mb_up bias_up
            var_up std_up rstd_up tanh_up rkm_up xn_up xt_ps xnT_sb kv_ps v_sb k_rope kh_up kl_up
            kt_ps k2_sb k1_sb q_ps q_rope qh_up ql_up qt_ps q2_sb q1_sb
            pa_ps pa_seen pa_max pm_red m16_up mt_ps mT_sb st_ps st_half bias_done e_up pv_ps sum_up o_sb den_ps
            rden_up on_up wo_ps y_up
            f_stats f_std f_rstd f_xn f_xt_ps f_xT_act f_xT_dve f_lg_ps f_lg f_sub f_exp f_gate
            f_h_ps f_gelu f_o_ps f_ob f_y""".split()
        s = {n: sem(n) for n in names}
        mbrow_in = [sem(f"mbrow_in{g}") for g in range(HKV)]
        zrow_in = [sem(f"zrow_in{g}") for g in range(HKV)]
        block = ctx.enter_context(nc.Block())

        N_CONST = 11

        @block.sync
        def _(sp):
            sp.dma_start(X[:, :, :], x.rearrange("b (q p) d -> p (b q) d", p=128)).then_inc(s["x_in"], 16)
            sp.dma_start(mask_u8[:, :], mask).then_inc(s["x_in"], 16)
            for dst, src in ((ident[:, :], ident_in), (wkv_sb[:, :, :], wkv), (wq_sb[:, :], wq),
                             (rk[:, :, :, :], rope_k), (rq[:, :, :, :], rope_q), (wo_sb[:, :, :], wo2),
                             (gx[:, 0:1], g_x.partition_broadcast(128)), (gx[:, 1:2], g_f.partition_broadcast(128)),
                             (gate_sb[:, :], gateT), (b1_sb[:, :], b1T),
                             (far[:, :], bias_far.partition_broadcast(128))):
                sp.dma_start(dst, src).then_inc(s["const_in"], 16)
            sp.wait_ge(s["init_pool"], 1)
            sp.dma_start(ctx_sb[:, 0:S2], ctxT[0, :, :]).then_inc(s["ctx_in"], 16)
            sp.dma_start(WB[:, :, :], bass.AP(tensor=bias_f.tensor, offset=bias_f.offset,
                                              ap=[[1, 128], [bias_f.shape[1], H], [1, WIN]])).then_inc(s["bias_in"], 16)
            sp.wait_ge(s["init_pool"], 5)
            for g in range(HKV):
                sp.dma_start(K1[D:D + 1, g, :], onerow[:, :]).then_inc(s["rows_in"], 16)
                sp.dma_start(Q1[D + 1:D + 2, g, :], bigrow[:, :]).then_inc(s["rows_in"], 16)

            def mask_row(P):
                if P.is_at_least(HKV):
                    sp.wait_ge(s["st_ps"], P.count(KT, -3 * KT))
                    sp.dma_start(Q1[D:D + 1, P.g, :], zero_dram).then_inc(zrow_in[P.g], 16)
                sp.dma_start(K1[D + 1:D + 2, P.g, :], mb_dram[ds(P.batch(), 1), :]).then_inc(mbrow_in[P.g], 16)

            def max_row(A):
                sp.wait_ge(s["mT_sb"], A.count(1, 1))
                sp.dma_start(Q1[D:D + 1, A.g, :].rearrange("o (a b) -> o a b", b=128), mT[:, :])\
                  .then_inc(s["mrow_in"], 16)

            def unit(u):
                if u.g == 1 and u.is_at_most(UNITS - 4):
                    sp.wait_ge(s["kv_ps"], u.count(4, 4 * 3))
                    sp.dma_start(ctx_sb[:, 0:S2], ctxT[ds(u.batch(1, 1), 1), :, :].rearrange("o d k -> (o d) k"))\
                      .then_inc(s["ctx_in"], 16)
                if u.is_at_most(UNITS - 4):
                    mask_row(u.at(3))
                if u.is_at_most(UNITS - 2):
                    max_row(u.at(1))

            sp.wait_ge(s["mb_up"], 3)
            sp.dma_start(mb_dram, mb16[:, :]).then_inc(s["mb_out"], 16)
            sp.wait_ge(s["mb_out"], 16)
            for P in range(3):
                mask_row(Unit(None, P))
            max_row(Unit(None, 0))
            unit(Unit(None, 0))
            with sp.Fori(0, B - 1) as b:
                for i in range(1, HKV + 1):
                    unit(Unit(b, i))
            for i in range(UNITS - 3, UNITS):
                unit(Unit(None, i))
            sp.wait_ge(s["bias_done"], (NEAR + 1) * UNITS)
            sp.wait_ge(s["pv_ps"], KT * UNITS)
            sp.dma_start(b2_sb[:, :, :], b2.partition_broadcast(128)).then_inc(s["ffw_in"], 16)
            sp.dma_start(W1.rearrange("p (e h) -> p e h", e=NE), w1.rearrange("e d h -> d e h")).then_inc(s["ffw_in"], 16)
            sp.dma_start(W2, w2).then_inc(s["ffw_in"], 16)
            with sp.Fori(0, TT // TG) as t:
                sp.wait_ge(s["f_y"], t * (NE * TG) + NE * TG)
                sp.dma_start(out[ds(t * (TG // QT), TG // QT), :, :].rearrange("b (q p) d -> p (b q) d", p=128),
                             X[:, ds(t * TG, TG), :]).then_inc(s["out_done"], 16)
            sp.wait_ge(s["out_done"], 16 * (TT // TG))

        def mask_rope(e, bt):
            m = maskT[:, ds(bt, 1), :].rearrange("p o t -> p (o t)").unsqueeze(2).broadcast_to([128, KT, 2 * D])
            return e.tensor_tensor(rkm[:, :, :, :].rearrange("p t a d -> p t (a d)"),
                                   rk[:, :, :, :].rearrange("p t a d -> p t (a d)"), m, ALU.mult)

        @block.gpsimd
        def _(pool):
            pool.memset(ctx_sb[:, S2:KP], 0.0).then_inc(s["init_pool"], 1)
            for n, (dst, value) in enumerate(((K1[D:128, :, :], 0.0), (Q1[D:128, :, :], 0.0), (onerow, 1.0),
                                              (bigrow, BIG_Q))):
                pool.wait_ge(s["init_pool"], n + 1)
                pool.memset(dst, value).then_inc(s["init_pool"], 1)

            def add(u, t):
                if t == 0:
                    return
                n = KT * u.g + t
                acc = esum[:, u.g % 2, :]
                pool.wait_ge(s["e_up"], u.count(KT, t + 1))
                if t == 1:
                    if u.is_at_least(2):
                        pool.wait_ge(s["den_ps"], u.count(1, -1))
                    pool.tensor_tensor(acc, E[:, (n - 1) % ERING, :], E[:, n % ERING, :], ALU.add)\
                        .then_inc(s["sum_up"], 1)
                else:
                    pool.wait_ge(s["sum_up"], u.count(KT - 1, t - 1))
                    pool.tensor_tensor(acc, acc, E[:, n % ERING, :], ALU.add).then_inc(s["sum_up"], 1)

            def k_low(P, r):
                t0, n = KTR[r]
                pool.wait_ge(s["kh_up"], P.count(2, r + 1))
                pool.tensor_tensor(khl[:, t0:t0 + n, D:2 * D], kr[:, t0:t0 + n, :], khl[:, t0:t0 + n, 0:D],
                                   ALU.subtract).then_inc(s["kl_up"], 1)

            def unit(u):
                for t in range(KT):
                    add(u, t)
                    if t in (7, 9) and u.is_at_most(UNITS - 4):
                        k_low(u.at(3), t // 2 - 3)
                    if t == 0 and u.g == 1 and u.is_at_most(UNITS - 4):
                        pool.wait_ge(s["k_rope"], u.count(16, 48))
                        mask_rope(pool, u.batch(1, 1)).then_inc(s["rkm_up"], 1)

            for P in range(3):
                for r in range(2):
                    k_low(Unit(None, P), r)
            unit(Unit(None, 0))
            with pool.Fori(0, B - 1) as b:
                for i in range(1, HKV + 1):
                    unit(Unit(b, i))
            for i in range(UNITS - 3, UNITS):
                unit(Unit(None, i))

        @block.scalar
        def _(act):
            act.wait_ge(s["var_up"], 1)
            act.activation(std[:, :], std[:, :], ACT.Sqrt).then_inc(s["std_up"], 1)
            act.wait_ge(s["const_in"], 16 * N_CONST)
            act.activation(tg_[:, :], gx[:, :], ACT.Tanh).then_inc(s["tanh_up"], 1)
            act.preload_act_table_set("natural_log_exp_and_others")

            def normalise(bt, n):
                if n is not None:
                    act.wait_ge(s["xt_ps"], n)
                for q in range(QT):
                    last = act.activation(xn[:, q, :], X[:, ds(bt * QT + q, 1), :].rearrange("p o d -> p (o d)"),
                                          ACT.Identity, bias=nmr[:, ds(bt * QT + q, 1)],
                                          scale=rstd[:, ds(bt * QT + q, 1)])
                last.then_inc(s["xn_up"], 1)

            def xt_out(n):
                act.wait_ge(s["xt_ps"], n)
                act.activation(xnT[:, :], mp[:, 0:M], ACT.Copy).then_inc(s["xnT_sb"], 1)

            def kv(P, r):
                t0, n = KV_ROUNDS[r]
                act.wait_ge(s["k_rope"], P.count(16, 4 * r + 3))
                if r == 0 and not P.is_at_least(1):
                    act.wait_ge(s["rows_in"], 16 * 2 * HKV)
                if r == 0 and P.is_at_least(HKV):
                    act.wait_ge(s["pv_ps"], P.count(KT, -3 * KT))
                act.activation(V[:, P.g, t0:t0 + n, :], mp_kv[:, 0:n, D:2 * D], ACT.Copy).then_inc(s["v_sb"], 1)

            def k_high(P, r):
                t0, n = KTR[r]
                act.wait_ge(s["k_rope"], P.count(16, 8 * r + 8))
                if r == 0 and P.is_at_least(1):
                    act.wait_ge(s["kt_ps"], P.count(2))
                act.activation(khl[:, t0:t0 + n, 0:D], kr[:, t0:t0 + n, :], ACT.Copy).then_inc(s["kh_up"], 1)

            def q_high(P):
                act.wait_ge(s["q_rope"], P.count(4, 4))
                if P.is_at_least(1):
                    act.wait_ge(s["qt_ps"], P.count(1))
                act.activation(qhl[:, :, :, D:2 * D], qr[:, :, :, :], ACT.Copy).then_inc(s["qh_up"], 1)

            def k_out(P, r):
                t0, n = KTR[r]
                act.wait_ge(s["kt_ps"], P.count(2, r + 1))
                if r == 0 and P.is_at_least(HKV):
                    act.wait_ge(s["st_ps"], P.count(KT, -3 * KT))
                act.activation(K1[0:D, P.g, t0 * 128:(t0 + n) * 128], mp16[0:D, 0:n * 128], ACT.Copy)\
                   .then_inc(s["k1_sb"], 1)
                act.activation(K2[:, P.g, t0 * 128:(t0 + n) * 128], mp16[:, 0:n * 128], ACT.Copy)\
                   .then_inc(s["k2_sb"], 1)

            def q_out(P):
                act.wait_ge(s["qt_ps"], P.count(1, 1))
                act.activation(Q1[0:D, P.g, :], mp16[D:2 * D, 0:UC], ACT.Copy).then_inc(s["q1_sb"], 1)
                act.activation(Q2[:, P.g, :], mp16[:, 0:UC], ACT.Copy).then_inc(s["q2_sb"], 1)

            def exp(u, t):
                n = KT * u.g + t
                if t < NEAR:
                    act.wait_ge(s["bias_done"], u.count(NEAR + 1, t + 2))
                else:
                    act.wait_ge(s["st_ps"], u.count(KT, t + 1))
                if not (u.reg is None and u.c == 0 and t < ERING):
                    act.wait_ge(s["pv_ps"], u.count(KT, t - ERING + 1))
                    k = t - ERING
                    off = max(k, 1) if k >= 0 else k + KT - (KT - 1)
                    act.wait_ge(s["sum_up"], u.count(KT - 1, off))
                act.activation(E[:, n % ERING, :], stp[n % 2][:, :], ACT.Exp).then_inc(s["e_up"], 1)

            def o_out(u):
                act.wait_ge(s["pv_ps"], u.count(KT, KT))
                if u.is_at_least(1):
                    act.wait_ge(s["wo_ps"], u.count(1))
                act.activation(oraw[:, :], op[:, :], ACT.Copy).then_inc(s["o_sb"], 1)

            def prep_round(P, r):
                if r < 4:
                    kv(P, r)
                if r in (2, 4):
                    k_high(P, r // 2 - 1)
                if r == 5:
                    q_high(P)
                if r in (5, 6):
                    k_out(P, r - 5)
                if r == 7:
                    q_out(P)

            def den(u):
                act.wait_ge(s["den_ps"], u.count(1, 1))
                if u.is_at_least(1):
                    act.wait_ge(s["on_up"], u.count(1))
                act.activation(rden[:, :], mp[:, :], ACT.Ln, scale=SUM_UNIT).then_inc(s["rden_up"], 1)
                act.wait_ge(s["rden_up"], u.count(2, 1))
                act.activation(rden[:, :], rden[:, :], ACT.Exp, scale=-1.0).then_inc(s["rden_up"], 1)

            def unit(u):
                P = u.at(3)
                prep = u.is_at_most(UNITS - 4)
                for t in range(KT):
                    if t == KT - 1:
                        o_out(u)
                    next_x = t == 0 and u.g == 1 and prep
                    if next_x:
                        normalise(u.batch(1, 1), u.batch(1, 1))
                    if t + 1 < KT:
                        exp(u, t + 1)
                    elif u.is_at_most(UNITS - 2):
                        exp(u.at(1), 0)
                    if next_x:
                        xt_out(u.batch(1, 2))
                    if t == 1 and u.is_at_least(1):
                        den(u.at(-1))
                    if prep:
                        if 4 <= t < 12:
                            prep_round(P, t - 4)

            act.wait_ge(s["rstd_up"], TT + 2)
            normalise(0, None)
            xt_out(1)
            for P in range(3):
                for r in range(8):
                    prep_round(Unit(None, P), r)
            exp(Unit(None, 0), 0)
            unit(Unit(None, 0))
            with act.Fori(0, B - 1) as b:
                for i in range(1, HKV + 1):
                    unit(Unit(b, i))
            for i in range(UNITS - 3, UNITS):
                unit(Unit(None, i))
            den(Unit(None, UNITS - 1))

            act.wait_ge(s["f_stats"], 2 * TT + 1)
            act.activation(std[:, :], std[:, :], ACT.Sqrt).then_inc(s["f_std"], 1)
            act.nop().then_inc(s["f_xT_act"], 1)
            with act.Fori(0, TT // TG) as t:
                act.wait_ge(s["f_xt_ps"], t + 2)
                act.activation(xTs, stp[0][:, 0:512], ACT.Copy).then_inc(s["f_xT_act"], 1)
            act.wait_ge(s["f_sub"], 2)
            act.activation(pr[:, :, :], lg[:, :, :], ACT.Exp).then_inc(s["f_exp"], 1)
            act.nop().then_inc(s["f_gelu"], HC)
            with act.Fori(0, TT // TG) as t:
                for e in range(NE):
                    for c in range(HC):
                        k = e * HC + c
                        act.wait_ge(s["f_h_ps"], t * (NE * HC) + k + 1)
                        if c == 0:
                            act.wait_ge(s["f_o_ps"], t * NE + e + 1)
                        act.activation(hid[:, ((e % 2) * HC + c) * 512:((e % 2) * HC + c + 1) * 512],
                                       stp[k // 2 % 2][:, 512 * (k % 2):512 * (k % 2) + 512], ACT.Gelu,
                                       bias=b1_sb[:, k:k + 1]).then_inc(s["f_gelu"], 1)

        @block.tensor
        def _(pe):
            pe.wait_ge(s["const_in"], 16 * N_CONST)
            pe.wait_ge(s["ident_up"], 1)
            pe.wait_ge(s["init_dve"], 1)
            pe.wait_ge(s["mask_f_up"], 2)
            for t in range(KT):
                last = pe.transpose(mp[:, t * B:(t + 1) * B], mask_f[:, t * 128:(t + 1) * 128], ident[0:B, 0:B])
            last.then_inc(s["mask_ps"], 1)
            pe.wait_ge(s["mask_sb"], 1)
            pe.wait_ge(s["any_up"], 2)
            pe.matmul(mp[:, 0:B], ones[0:B, :], diag16[:, :], start=True, stop=True).then_inc(s["any_ps"], 1)
            pe.wait_ge(s["any_sb"], 1)

            def xt(b_sem):
                pe.wait_ge(s["xn_up"], b_sem)
                for q in range(QT):
                    last = pe.transpose(mp[:, q * 128:(q + 1) * 128], xn[:, q, :], ident[:, :])
                last.then_inc(s["xt_ps"], 1)

            def kv(P, r):
                t0, n = KV_ROUNDS[r]
                if r:
                    pe.wait_ge(s["v_sb"], P.count(4, r))
                    pe.wait_ge(s["k_rope"], P.count(16, 4 * r - 1))
                else:
                    pe.wait_ge(s["ctx_in"], P.batch(16, 16))
                for j in range(n):
                    last = pe.matmul(mp_kv[:, j, :], ctx_sb[:, (t0 + j) * 128:(t0 + j + 1) * 128],
                                     wkv_sb[:, P.g, :], start=True, stop=True)
                last.then_inc(s["kv_ps"], 1)

            def q_proj(P):
                pe.wait_ge(s["v_sb"], P.count(4, 4))
                pe.wait_ge(s["k_rope"], P.count(16, 15))
                pe.wait_ge(s["xnT_sb"], P.batch(1, 1))
                for q in range(QT):
                    last = pe.matmul(mp[:, q * 256:(q + 1) * 256], xnT[:, q * 128:(q + 1) * 128],
                                     wq_sb[:, P.g * G * D:(P.g + 1) * G * D], start=True, stop=True)
                last.then_inc(s["q_ps"], 1)

            def k_turn(P, r):
                t0, n = KTR[r]
                if r:
                    pe.wait_ge(s["k2_sb"], P.count(2, 1))
                    pe.wait_ge(s["k1_sb"], P.count(2, 1))
                else:
                    pe.wait_ge(s["q_rope"], P.count(4, 3))
                pe.wait_ge(s["kh_up"], P.count(2, r + 1))
                pe.wait_ge(s["kl_up"], P.count(2, r + 1))
                for j in range(n):
                    last = pe.transpose(mp16[:, j * 128:(j + 1) * 128], khl[:, t0 + j, :], ident16[:, :])
                last.then_inc(s["kt_ps"], 1)

            def q_turn(P):
                pe.wait_ge(s["k2_sb"], P.count(2, 2))
                pe.wait_ge(s["k1_sb"], P.count(2, 2))
                pe.wait_ge(s["qh_up"], P.count(1, 1))
                pe.wait_ge(s["ql_up"], P.count(1, 1))
                for j in range(G):
                    for q in range(QT):
                        c = (j * QT + q) * 128
                        last = pe.transpose(mp16[:, c:c + 128], qhl[:, q, j, :], ident16[:, :])
                last.then_inc(s["qt_ps"], 1)

            def turned(n):
                pe.wait_ge(s["q1_sb"], n)
                pe.wait_ge(s["q2_sb"], n)

            def chunk(A, i):
                if i == 0:
                    turned(A.count(1, 1))
                    pe.wait_ge(s["k1_sb"], A.count(2, 2))
                    pe.wait_ge(mbrow_in[A.g], A.batch(16, 16))
                    if A.is_at_least(HKV):
                        pe.wait_ge(zrow_in[A.g], A.batch(16))
                    else:
                        pe.wait_ge(s["rows_in"], 16 * 2 * HKV)
                if not (A.reg is None and A.c == 0 and i < 2):
                    pe.wait_ge(s["pa_max"], A.count(PA, i - 1))
                hq, c = divmod(i, NCH)
                k0, n, _ = CHUNKS[c]
                pe.matmul(pap[i % 2][:, 0:n], Q1[:, A.g, hq * 128:(hq + 1) * 128], K1[:, A.g, k0:k0 + n],
                          start=True, stop=True).then_inc(s["pa_ps"], 1)

            def m_turn(A):
                pe.wait_ge(s["m16_up"], A.count(1, 1))
                pe.transpose(mp16[0:G * QT, 0:128], m16[:, :], ident16[:, :]).then_inc(s["mt_ps"], 1)

            def scores(u, t, hf):
                n = KT * u.g + t
                if t == 0 and hf == 0:
                    pe.wait_ge(s["mrow_in"], u.count(16, 16))
                    pe.wait_ge(s["k2_sb"], u.count(2, 2))
                if hf == 0 and not (u.reg is None and u.c == 0 and t < 2):
                    pe.wait_ge(s["e_up"], u.count(KT, t - 1))
                cols = slice(hf * 512, hf * 512 + 512)
                pe.matmul(stp[n % 2][:, cols], K1[:, u.g, t * 128:(t + 1) * 128], Q1[:, u.g, cols],
                          start=True, stop=False)
                last = pe.matmul(stp[n % 2][:, cols], K2[:, u.g, t * 128:(t + 1) * 128], Q2[:, u.g, cols],
                                 start=False, stop=True)
                if hf == 1:
                    last.then_inc(s["st_ps"], 1)
                elif t == 0:
                    last.then_inc(s["st_half"], 1)

            def pv(u, t):
                n = KT * u.g + t
                pe.wait_ge(s["e_up"], u.count(KT, t + 1))
                if t == 0 and u.is_at_least(1):
                    pe.wait_ge(s["o_sb"], u.count(1))
                for hf in range(2):
                    last = pe.matmul(op[hf * 64:hf * 64 + 64, :], V[:, u.g, t, :],
                                     E[:, n % ERING, hf * 512:hf * 512 + 512], start=(t == 0), stop=(t == KT - 1))
                last.then_inc(s["pv_ps"], 1)

            def den(u):
                pe.wait_ge(s["sum_up"], u.count(KT - 1, KT - 1))
                for hf in range(2):
                    last = pe.matmul(mp[hf * 64:hf * 64 + 64, :], ones[:, 0:64],
                                     esum[:, u.g % 2, hf * 512:hf * 512 + 512], start=True, stop=True)
                last.then_inc(s["den_ps"], 1)

            def out_proj(u):
                pe.wait_ge(s["on_up"], u.count(1, 1))
                for q in range(QT):
                    for hh in range(2):
                        last = pe.matmul(mp[:, q * 128:(q + 1) * 128],
                                         onorm[:, hh * 256 + q * 128:hh * 256 + (q + 1) * 128],
                                         wo_sb[:, u.g * 2 + hh, :], start=(hh == 0), stop=(hh == 1))
                last.then_inc(s["wo_ps"], 1)

            def prep_round(P, r):
                if r < 4:
                    kv(P, r)
                if r == 4:
                    q_proj(P)
                if r in (5, 6):
                    k_turn(P, r - 5)
                if r == 7:
                    q_turn(P)

            def unit(u):
                P, A = u.at(3), u.at(2)
                prep, passa = u.is_at_most(UNITS - 4), u.is_at_most(UNITS - 3)
                for t in range(KT):
                    for hf in range(2):
                        if passa and hf < PA_STEPS[t]:
                            chunk(A, PA_FROM[t] + hf)
                        if t + 1 < KT:
                            scores(u, t + 1, hf)
                        elif u.is_at_most(UNITS - 2):
                            scores(u.at(1), 0, hf)
                    if passa:
                        for i in range(PA_FROM[t] + 2, PA_FROM[t + 1]):
                            chunk(A, i)
                    if t == 0 and u.g == 1 and prep:
                        turned(P.count(1))
                        xt(u.batch(1, 2))
                    if t == 1 and u.is_at_least(1):
                        if u.is_at_most(UNITS - 3):
                            turned(P.count(1))
                        if u.g == 1 and prep:
                            pe.wait_ge(s["xnT_sb"], u.batch(1, 2))
                        if u.is_at_least(2):
                            pe.wait_ge(s["y_up"], u.count(1, -1))
                        den(u.at(-1))
                    if t == 2 and u.is_at_most(UNITS - 2):
                        if u.is_at_least(1):
                            pe.wait_ge(s["rden_up"], u.count(2, -1))
                        else:
                            turned(3)
                        m_turn(u.at(1))
                    if t == 3 and u.is_at_least(1):
                        if u.is_at_most(UNITS - 2):
                            pe.wait_ge(s["mT_sb"], u.count(1, 2))
                        else:
                            pe.wait_ge(s["rden_up"], u.count(2, -1))
                        out_proj(u.at(-1))
                    if prep:
                        if t == 4:
                            if u.is_at_least(1):
                                pe.wait_ge(s["y_up"], u.count(1))
                            else:
                                pe.wait_ge(s["mT_sb"], 2)
                        if 4 <= t < 12:
                            prep_round(P, t - 4)
                    pv(u, t)

            xt(1)
            pe.wait_ge(s["xnT_sb"], 1)
            for P in range(3):
                for r in range(8):
                    if P:
                        for i in range(4 * r, 4 * r + 4):
                            chunk(Unit(None, P - 1), i)
                    if r == 0 and P == 1:
                        turned(1)
                    if r == 0 and P == 2:
                        pe.wait_ge(s["mT_sb"], 1)
                    prep_round(Unit(None, P), r)
                if P == 1:
                    turned(2)
                    m_turn(Unit(None, 0))
            scores(Unit(None, 0), 0, 0)
            scores(Unit(None, 0), 0, 1)
            unit(Unit(None, 0))
            with pe.Fori(0, B - 1) as b:
                for i in range(1, HKV + 1):
                    unit(Unit(b, i))
            for i in range(UNITS - 3, UNITS):
                unit(Unit(None, i))
            last_u = Unit(None, UNITS - 1)
            pe.wait_ge(s["y_up"], UNITS - 1)
            den(last_u)
            pe.wait_ge(s["rden_up"], 2 * UNITS - 1)
            out_proj(last_u)

            pe.nop().then_inc(s["f_xt_ps"], 1)
            with pe.Fori(0, TT // TG) as t:
                pe.wait_ge(s["f_xn"], t + 1)
                pe.wait_ge(s["f_xT_dve"], t + 1)
                pe.wait_ge(s["f_xT_act"], t + 1)
                for j in range(TG):
                    last = pe.transpose(stp[0][:, j * 128:(j + 1) * 128], xn[:, j, :], ident[:, :])
                last.then_inc(s["f_xt_ps"], 1)
                pe.wait_ge(s["f_xT_act"], t + 2)
                pe.wait_ge(s["f_lg"], t + 1)
                for j in range(TG):
                    last = pe.matmul(mp[:, j * NE:(j + 1) * NE], xTs[:, j * 128:(j + 1) * 128], gate_sb[:, :],
                                     start=True, stop=True)
                last.then_inc(s["f_lg_ps"], 1)

            pe.wait_ge(s["ffw_in"], 48)
            pe.wait_ge(s["f_xT_dve"], TT // TG + 1)

            def up(t, e):
                for c in range(HC):
                    k = e * HC + c
                    pe.wait_ge(s["f_gelu"], t * (NE * HC) + k + 1)
                    pe.matmul(stp[k // 2 % 2][:, 512 * (k % 2):512 * (k % 2) + 512], W1[:, k * 128:(k + 1) * 128],
                              XT2[:, ds(t * 512, 512)], start=True, stop=True).then_inc(s["f_h_ps"], 1)

            def down(t, e):
                pe.wait_ge(s["f_gelu"], t * (NE * HC) + (e + 2) * HC)
                pe.wait_ge(s["f_ob"], t * NE + e + 1)
                for j in range(TG):
                    for c in range(HC):
                        a = ((e % 2) * HC + c) * 512 + j * 128
                        last = pe.matmul(pap[e % 2][:, j * 128:(j + 1) * 128], hid[:, a:a + 128],
                                         W2[:, (e * HC + c) * 128:(e * HC + c + 1) * 128],
                                         start=(c == 0), stop=(c == HC - 1))
                last.then_inc(s["f_o_ps"], 1)

            pe.nop().then_inc(s["f_o_ps"], 2)
            with pe.Fori(0, TT // TG) as t:
                up(t, 0)
                for e in range(NE):
                    if e + 1 < NE:
                        up(t, e + 1)
                    down(t, e)

        @block.vector
        def _(dve):
            dve.memset(ones[:, :], 1.0).then_inc(s["init_dve"], 1)
            dve.memset(mask_f, 0.0).then_inc(s["mask_f_up"], 1)
            dve.memset(mb16[:, S2:KP], BIG_K).then_inc(s["mb_up"], 1)
            dve.wait_ge(s["x_in"], 32)
            dve.wait_ge(s["mask_f_up"], 1)
            dve.tensor_copy(mask_f[:, 0:S2], mask_u8[:, :]).then_inc(s["mask_f_up"], 1)
            for j in range(TT):
                dve.bn_stats(stats[:, j, :], X[:, j, :]).then_inc(s["f_stats"], 1)
            dve.wait_ge(s["mask_f_up"], 2)
            dve.tensor_reduce(any16[:, :], mask_f, AX.X, ALU.max).then_inc(s["any_up"], 1)
            dve.tensor_scalar(mask_t, mask_f, -1.0, -BIG_K, ALU.add, ALU.mult).then_inc(s["mb_up"], 1)
            for j in range(TT):
                dve.wait_ge(s["f_stats"], j + 1)
                dve.bn_aggr(mv[:, j, :], stats[:, j, :]).then_inc(s["rstd_up"], 1)
            dve.wait_ge(s["rstd_up"], TT)
            dve.tensor_scalar(std[:, :], mv[:, :, 1], 1e-5, None, ALU.add).then_inc(s["var_up"], 1)
            dve.wait_ge(s["const_in"], 16 * N_CONST)
            dve.tensor_copy(ident16[:, :], ident[:, :]).then_inc(s["ident_up"], 1)
            dve.wait_ge(s["any_up"], 1)
            dve.tensor_scalar(diag16[:, :], ident[0:B, 0:B], any16[:, 0:1], None, ALU.mult).then_inc(s["any_up"], 1)
            dve.wait_ge(s["mb_up"], 2)
            dve.tensor_scalar(mb16[:, 0:S2], mask_t[:, 0:S2], any16[:, 0:1], None, ALU.mult).then_inc(s["mb_up"], 1)
            dve.wait_ge(s["mask_ps"], 1)
            dve.tensor_copy(maskT[:, :, :].rearrange("p b t -> p t b"),
                            mp[:, 0:KT * B].rearrange("p (t b) -> p t b", t=KT)).then_inc(s["mask_sb"], 1)
            dve.wait_ge(s["any_ps"], 1)
            dve.tensor_copy(anyb[:, :], mp[:, 0:B]).then_inc(s["any_sb"], 1)
            dve.wait_ge(s["std_up"], 1)
            dve.reciprocal(rstd[:, :], std[:, :]).then_inc(s["rstd_up"], 1)
            dve.wait_ge(s["rstd_up"], TT + 1)
            dve.scalar_tensor_tensor(nmr[:, :], mv[:, :, 0], -1.0, rstd[:, :], ALU.mult, ALU.mult)\
               .then_inc(s["rstd_up"], 1)
            dve.wait_ge(s["mask_sb"], 1)

            def kv(P, r):
                t0, n = KV_ROUNDS[r]
                if r == 0:
                    dve.wait_ge(s["rkm_up"], P.batch(1, 1))
                    if P.is_at_least(1):
                        dve.wait_ge(s["kh_up"], P.count(2))
                        dve.wait_ge(s["kl_up"], P.count(2))
                if not (P.reg is None and P.c == 0 and r == 0):
                    dve.wait_ge(s["k_rope"], P.count(16, 4 * r))
                dve.wait_ge(s["kv_ps"], P.count(4, r + 1))
                h = D // 2
                dve.tensor_tensor(kt1[:, 0:n, :], mp_kv[:, 0:n, 0:D], rkm[:, t0:t0 + n, 0, :], ALU.mult)\
                   .then_inc(s["k_rope"], 1)
                dve.tensor_tensor(kt2[:, 0:n, 0:h], mp_kv[:, 0:n, h:D], rkm[:, t0:t0 + n, 1, 0:h], ALU.mult)\
                   .then_inc(s["k_rope"], 1)
                dve.tensor_tensor(kt2[:, 0:n, h:D], mp_kv[:, 0:n, 0:h], rkm[:, t0:t0 + n, 1, h:D], ALU.mult)\
                   .then_inc(s["k_rope"], 1)
                dve.wait_ge(s["k_rope"], P.count(16, 4 * r + 3))
                dve.tensor_tensor(kr[:, t0:t0 + n, :], kt1[:, 0:n, :], kt2[:, 0:n, :], ALU.add)\
                   .then_inc(s["k_rope"], 1)

            def q_rope(P):
                h = D // 2
                dve.wait_ge(s["q_ps"], P.count(1, 1))
                if P.is_at_least(1):
                    dve.wait_ge(s["q_rope"], P.count(4))
                    dve.wait_ge(s["qh_up"], P.count(1))
                    dve.wait_ge(s["ql_up"], P.count(1))
                m = mp[:, :].rearrange("p (q j d) -> p q j d", q=QT, j=G)
                cos = rq[:, :, 0:1, :].broadcast_to([128, QT, G, D])
                dve.tensor_tensor(qt1[:, :, :, :], m, cos, ALU.mult).then_inc(s["q_rope"], 1)
                dve.tensor_tensor(qt2[:, :, :, 0:h], m[:, :, :, h:D],
                                  rq[:, :, 1:2, 0:h].broadcast_to([128, QT, G, h]), ALU.mult).then_inc(s["q_rope"], 1)
                dve.tensor_tensor(qt2[:, :, :, h:D], m[:, :, :, 0:h],
                                  rq[:, :, 1:2, h:D].broadcast_to([128, QT, G, h]), ALU.mult).then_inc(s["q_rope"], 1)
                dve.wait_ge(s["q_rope"], P.count(4, 3))
                dve.tensor_tensor(qr[:, :, :, :], qt1[:, :, :, :], qt2[:, :, :, :], ALU.add).then_inc(s["q_rope"], 1)

            def q_low(P):
                dve.wait_ge(s["qh_up"], P.count(1, 1))
                dve.tensor_tensor(qhl[:, :, :, 0:D], qr[:, :, :, :], qhl[:, :, :, D:2 * D], ALU.subtract)\
                   .then_inc(s["ql_up"], 1)

            def prep_round(P, r):
                if r < 4:
                    kv(P, r)
                if r == 4:
                    q_rope(P)
                if r == 5:
                    q_low(P)

            def chunk(A, i):
                hq, c = divmod(i, NCH)
                j, q = divmod(hq, QT)
                k0, n, with_bias = CHUNKS[c]
                if i == 0 and A.is_at_least(1):
                    dve.wait_ge(s["pm_red"], A.count(1))
                dve.wait_ge(s["pa_ps"], A.count(PA, i + 1))
                if with_bias:
                    a = 128 * q + k0
                    if not (A.reg is None and A.c == 0 and i < 2):
                        dve.wait_ge(s["pa_max"], A.count(PA, i - 1))
                    dve.sem_inc(s["pa_seen"], 1)
                    dve.tensor_tensor_reduce(junk[:, i % 2, :], pap[i % 2][:, 0:n], WB[:, A.g * G + j, a:a + n], 1.0,
                                             -3.0e38, ALU.add, ALU.max, pm[:, hq, c:c + 1]).then_inc(s["pa_max"], 1)
                else:
                    dve.tensor_reduce(pm[:, hq, c:c + 1], pap[i % 2][:, 0:n], AX.X, ALU.max)\
                       .then_inc(s["pa_max"], 1)

            def maxima(A):
                dve.wait_ge(s["pa_max"], A.count(PA, PA))
                if A.is_at_least(1):
                    dve.wait_ge(s["m16_up"], A.count(1))
                dve.tensor_reduce(mred[:, :], pm[:, :, :], AX.X, ALU.max).then_inc(s["pm_red"], 1)
                dve.wait_ge(s["pm_red"], A.count(1, 1))
                if A.is_at_least(1):
                    dve.wait_ge(s["mt_ps"], A.count(1))
                dve.tensor_scalar(m16[:, :], mred[:, :], anyb[:, ds(A.batch(), 1)], -1.0, ALU.mult, ALU.mult)\
                   .then_inc(s["m16_up"], 1)

            def m_out(A):
                dve.wait_ge(s["mt_ps"], A.count(1, 1))
                if A.is_at_least(1):
                    dve.wait_ge(s["mrow_in"], A.count(16))
                dve.tensor_copy(mT[:, :], mp16[0:G * QT, 0:128]).then_inc(s["mT_sb"], 1)

            def bias(u, t):
                n = KT * u.g + t
                halves = 2 if t == 0 else 1
                for hf in range(halves):
                    if hf == 0 and t == 0:
                        dve.wait_ge(s["st_half"], u.count(1, 1))
                    else:
                        dve.wait_ge(s["st_ps"], u.count(KT, t + 1))
                    j0, nj = hf * G // halves, G // halves
                    p3 = stp[n % 2][:, j0 * M:(j0 + nj) * M].rearrange("p (j i) -> p j i", j=nj)
                    dve.scalar_tensor_tensor(p3, WB[:, u.g * G + j0:u.g * G + j0 + nj, t * 128:t * 128 + M],
                                             maskT[:, ds(u.batch(), 1), t:t + 1].rearrange("p o t -> p (o t)"), p3,
                                             ALU.mult, ALU.add).then_inc(s["bias_done"], 1)

            def den(u):
                dve.wait_ge(s["rden_up"], u.count(2, 2))
                dve.wait_ge(s["o_sb"], u.count(1, 1))
                dve.tensor_tensor(onorm[:, :], oraw[:, :], rden[:, :], ALU.mult).then_inc(s["on_up"], 1)

            def residual(u):
                dve.wait_ge(s["wo_ps"], u.count(1, 1))
                if u.is_at_least(1):
                    dve.wait_ge(s["y_up"], u.count(1))
                xs = X[:, ds(u.batch(QT), QT), :].rearrange("p q d -> p (q d)")
                dve.scalar_tensor_tensor(xs, mp[:, 0:M], tg_[:, 0:1], xs, ALU.mult, ALU.add).then_inc(s["y_up"], 1)

            def unit(u):
                P, A = u.at(3), u.at(2)
                prep, passa = u.is_at_most(UNITS - 4), u.is_at_most(UNITS - 3)
                for t in range(KT):
                    first = min(2, PA_STEPS[t])
                    if passa:
                        for i in range(PA_FROM[t], PA_FROM[t] + first):
                            chunk(A, i)
                    if t + 1 < NEAR:
                        bias(u, t + 1)
                    elif t == KT - 1 and u.is_at_most(UNITS - 2):
                        bias(u.at(1), 0)
                    if t == 2 and u.is_at_least(1):
                        den(u.at(-1))
                    if passa:
                        for i in range(PA_FROM[t] + first, PA_FROM[t + 1]):
                            chunk(A, i)
                    if t == 2 and u.is_at_most(UNITS - 2):
                        m_out(u.at(1))
                    if t == 3 and u.is_at_least(1):
                        residual(u.at(-1))
                    if prep:
                        if 4 <= t < 12:
                            prep_round(P, t - 4)
                    if t == 12 and passa:
                        maxima(A)

            mask_rope(nc.vector, 0).then_inc(s["rkm_up"], 1)
            dve.wait_ge(s["bias_in"], 16)
            for h in range(H):
                dve.tensor_scalar(WB[:, h, :], WB[:, h, :], far[:, h:h + 1], None, ALU.subtract)\
                   .then_inc(s["bias_up"], 1)
            dve.wait_ge(s["bias_up"], H)
            dve.wait_ge(s["any_sb"], 1)
            dve.wait_ge(s["tanh_up"], 1)
            dve.tensor_scalar(tg_[:, 0:1], tg_[:, 0:1], SUM_UNIT, None, ALU.mult).then_inc(s["tanh_up"], 1)
            dve.wait_ge(s["tanh_up"], 2)
            for P in range(3):
                for r in range(8):
                    if P:
                        for i in range(4 * r, 4 * r + 4):
                            chunk(Unit(None, P - 1), i)
                    prep_round(Unit(None, P), r)
                if P:
                    maxima(Unit(None, P - 1))
                if P == 1:
                    m_out(Unit(None, 0))
            bias(Unit(None, 0), 0)
            unit(Unit(None, 0))
            with dve.Fori(0, B - 1) as b:
                for i in range(1, HKV + 1):
                    unit(Unit(b, i))
            for i in range(UNITS - 3, UNITS):
                unit(Unit(None, i))
            last_u = Unit(None, UNITS - 1)
            den(last_u)
            residual(last_u)

            dve.wait_ge(s["y_up"], UNITS)
            for j in range(TT):
                dve.bn_stats(stats[:, j, :], X[:, j, :]).then_inc(s["f_stats"], 1)
            for j in range(TT):
                dve.wait_ge(s["f_stats"], TT + j + 1)
                dve.bn_aggr(mv[:, j, :], stats[:, j, :]).then_inc(s["f_rstd"], 1)
            dve.wait_ge(s["f_rstd"], TT)
            dve.tensor_scalar(std[:, :], mv[:, :, 1], 1e-5, None, ALU.add).then_inc(s["f_stats"], 1)
            dve.wait_ge(s["f_std"], 1)
            dve.reciprocal(rstd[:, :], std[:, :]).then_inc(s["f_rstd"], 1)
            dve.memset(iota_r[:, :], 0.0).then_inc(s["f_rstd"], 1)
            dve.wait_ge(s["f_rstd"], TT + 2)
            for e in range(NE):
                dve.memset(iota_r[:, e:e + 1], float(NE - e)).then_inc(s["f_rstd"], 1)
            dve.nop().then_inc(s["f_xT_dve"], 1)
            dve.nop().then_inc(s["f_lg"], 1)
            with dve.Fori(0, TT // TG) as t:
                dve.wait_ge(s["f_xt_ps"], t + 1)
                for j in range(TG):
                    last = dve.tensor_scalar(xn[:, j, :], X[:, ds(t * TG + j, 1), :].rearrange("p o d -> p (o d)"),
                                             mv[:, ds(t * TG + j, 1), 0:1].rearrange("p o d -> p (o d)"),
                                             rstd[:, ds(t * TG + j, 1)], ALU.subtract, ALU.mult)
                last.then_inc(s["f_xn"], 1)
                dve.wait_ge(s["f_xt_ps"], t + 2)
                dve.wait_ge(s["f_xT_act"], t + 2)
                dve.tensor_copy(XT2[:, ds(t * 512, 512)], stp[0][:, 0:512]).then_inc(s["f_xT_dve"], 1)
                dve.wait_ge(s["f_lg_ps"], t + 1)
                dve.tensor_copy(lg[:, ds(t * TG, TG), :], mp[:, 0:TG * NE].rearrange("p (j e) -> p j e", e=NE))\
                   .then_inc(s["f_lg"], 1)

            def wide(v):
                return v[:, :].unsqueeze(2).broadcast_to([128, TT, NE])

            g_count = [0]

            def gate(ins):
                g_count[0] += 1
                ins.then_inc(s["f_gate"], 1)
                dve.wait_ge(s["f_gate"], g_count[0])

            dve.wait_ge(s["f_lg"], TT // TG + 1)
            dve.tensor_reduce(r1[:, :], lg[:, :, :], AX.X, ALU.max).then_inc(s["f_sub"], 1)
            dve.wait_ge(s["f_sub"], 1)
            dve.tensor_tensor(lg[:, :, :], lg[:, :, :], wide(r1), ALU.subtract).then_inc(s["f_sub"], 1)
            dve.wait_ge(s["f_exp"], 1)
            gate(dve.tensor_reduce(r1[:, :], pr[:, :, :], AX.X, ALU.add))
            gate(dve.reciprocal(r2[:, :], r1[:, :]))
            gate(dve.tensor_tensor(pr[:, :, :], pr[:, :, :], wide(r2), ALU.mult))
            order = iota_r[:, :].unsqueeze(1).broadcast_to([128, TT, NE])

            def first_max(src, sel, best):
                gate(dve.tensor_reduce(best[:, :], src, AX.X, ALU.max))
                gate(dve.tensor_tensor(sel, src, wide(best), ALU.is_equal))
                gate(dve.tensor_tensor(sel, sel, order, ALU.mult))
                gate(dve.tensor_reduce(r3[:, :], sel, AX.X, ALU.max))
                gate(dve.tensor_tensor(sel, order, wide(r3), ALU.is_equal))

            first_max(pr[:, :, :], wsel[:, :, :], r1)
            gate(dve.tensor_scalar(ga[:, :, :], wsel[:, :, :], -2.0, None, ALU.mult))
            gate(dve.tensor_tensor(ga[:, :, :], ga[:, :, :], pr[:, :, :], ALU.add))
            first_max(ga[:, :, :], gb[:, :, :], r2)
            gate(dve.tensor_tensor(wsel[:, :, :], wsel[:, :, :], gb[:, :, :], ALU.add))
            gate(dve.tensor_tensor(wsel[:, :, :], wsel[:, :, :], pr[:, :, :], ALU.mult))
            gate(dve.scalar_tensor_tensor(r3[:, :], r1[:, :], 1e-9, r2[:, :], ALU.add, ALU.add))
            gate(dve.reciprocal(r1[:, :], r3[:, :]))
            gate(dve.tensor_tensor(wsel[:, :, :], wsel[:, :, :], wide(r1), ALU.mult))
            gate(dve.tensor_scalar(wsel[:, :, :], wsel[:, :, :], tg_[:, 1:2], None, ALU.mult))

            dve.nop().then_inc(s["f_ob"], 1)
            dve.wait_ge(s["ffw_in"], 48)
            with dve.Fori(0, TT // TG) as t:
                for e in range(NE):
                    dve.wait_ge(s["f_o_ps"], t * NE + e + 3)
                    o = oe[:, (e % 2) * 512:(e % 2) * 512 + 512].rearrange("p (j d) -> p j d", j=TG)
                    b2e = b2_sb[:, e:e + 1, :].broadcast_to([128, TG, DM])
                    dve.tensor_tensor(o, pap[e % 2][:, :].rearrange("p (j d) -> p j d", j=TG), b2e, ALU.add)\
                       .then_inc(s["f_ob"], 1)
                    dve.wait_ge(s["f_ob"], t * NE + e + 2)
                    for j in range(TG):
                        xs = X[:, ds(t * TG + j, 1), :].rearrange("p o d -> p (o d)")
                        w = wsel[:, ds(t * TG + j, 1), e:e + 1].rearrange("p o d -> p (o d)")
                        if e:
                            dve.wait_ge(s["f_y"], t * (NE * TG) + (e - 1) * TG + j + 1)
                        dve.scalar_tensor_tensor(xs, o[:, j, :], w, xs, ALU.mult, ALU.add).then_inc(s["f_y"], 1)


def _constants():
    import numpy as np
    inv = np.float32(1) / (np.float64(10000.0) ** (np.arange(0, D, 2, dtype=np.float32) / np.float32(D)).astype(np.float64)).astype(np.float32)

    def table(pos, scale):
        f = np.repeat(np.outer(pos.astype(np.float32), inv), 2, axis=-1)
        cos, sin = np.cos(f), np.sin(f)
        sin[:, :D // 2] *= -1
        return (np.stack([cos, sin], 1) * np.float32(scale)).astype(np.float32)

    rk = table(np.arange(KP), 1.0).reshape(KT, 128, 2, D).transpose(1, 0, 2, 3)
    rq = table(M - 1 - np.arange(M), D ** -0.5).reshape(QT, 128, 2, D).transpose(1, 0, 2, 3)
    return np.ascontiguousarray(rk), np.ascontiguousarray(rq), np.eye(128, dtype=np.float32)


def kernel(x, ctx_1024, mask_BxS2_bf1, g_xattn, g_ffn, L0_xattn_Wq, L0_xattn_Wk, L0_xattn_Wv, L0_xattn_Wo,
           L0_xattn_rel_pos_bias, L0_ffn_gate_w, L0_ffn_w1, L0_ffn_b1, L0_ffn_w2, L0_ffn_b2):
    import numpy as np
    import concourse.bacc as bacc
    from concourse.bass_utils import run_bass_kernel_spmd

    a = np.asarray
    c = np.ascontiguousarray
    rk, rq, eye = _constants()
    wk, wv, wo, bias = a(L0_xattn_Wk), a(L0_xattn_Wv), a(L0_xattn_Wo), a(L0_xattn_rel_pos_bias)
    wkv = np.concatenate([wk.reshape(DM, HKV, D), wv.reshape(DM, HKV, D)], axis=2)
    wo2 = wo.reshape(HKV, 2, 2, D, DM).transpose(1, 3, 0, 2, 4).reshape(128, HKV * 2, DM)
    dist = np.minimum(np.abs(np.arange(WIN + 127) - (M - 1)), MAXREL - 1)
    arrays = {
        "x": c(a(x)[:, ::-1, :]), "ctxT": c(a(ctx_1024).transpose(0, 2, 1)), "mask": c(a(mask_BxS2_bf1)).view(np.uint8),
        "g_x": c(a(g_xattn)), "g_f": c(a(g_ffn)), "wq": c(a(L0_xattn_Wq)), "wkv": c(wkv), "wo2": c(wo2),
        "bias_f": c(bias[:, dist]), "bias_far": c(bias[:, MAXREL - 1]), "gateT": c(a(L0_ffn_gate_w).T),
        "w1": c(a(L0_ffn_w1)), "b1T": c(a(L0_ffn_b1).reshape(NE * HC, 128).T),
        "w2": c(a(L0_ffn_w2).reshape(NE * HC, 128, DM).transpose(1, 0, 2).reshape(128, NE * HC * DM)), "b2": c(a(L0_ffn_b2)),
        "rope_k": rk, "rope_q": rq, "ident": eye,
        "zeros": np.zeros((1, UC), np.float16),
    }
    nc = bacc.Bacc("TRN2", target_bir_lowering=False, num_devices=1)
    args = [nc.dram_tensor(f"in_{k}", v.shape, mybir.dt.from_np(v.dtype), kind="ExternalInput").ap()
            for k, v in arrays.items()]
    out = nc.dram_tensor("out_0", [B, M, DM], mybir.dt.float32, kind="ExternalOutput").ap()
    flamingo_block(nc, *args, out)
    r = run_bass_kernel_spmd(nc, [{f"in_{k}": v for k, v in arrays.items()}], core_ids=[0])
    return r.results[0]["out_0"][:, ::-1, :]
```

```python
import concourse.bass as bass
from concourse import mybir
from contextlib import ExitStack

B, M, S2, DM = 16, 256, 1601, 128
H, HKV, D = 16, 4, 64
G = H // HKV
QT = M // 128
KT = (S2 + 127) // 128
KP = KT * 128
UNITS = B * HKV
UC = G * M
MAXREL = 384
NEAR = 5
WIN = (NEAR - 1) * 128 + M
SUM_UNIT = 2.0 ** -6
ERING = 4
NE, HID, TOPC = 8, 512, 2
HC = HID // 128
TT = B * QT
TG = 4
CTX_PARTS = [(0, (KT + 1) // 2 * 128), ((KT + 1) // 2 * 128, S2 - (KT + 1) // 2 * 128)]
NG = TT // TG
GC = TG * 128
SW = 64.0
BIG_Q, BIG_K = 32768.0, -30528.0
CHUNKS = [(0, 320, True), (320, 320, True), (640, 481, False), (1121, 480, False)]
NCH = len(CHUNKS)
PA = G * QT * NCH
PA_STEPS = [2, 2, 1, 2, 3, 3, 3, 3, 2, 3, 3, 3, 2]
assert sum(PA_STEPS) == PA and len(PA_STEPS) == KT
PA_FROM = [sum(PA_STEPS[:t]) for t in range(KT + 1)]
KV_ROUNDS = [(r, min(4, KT - r)) for r in range(0, KT, 4)]
KTR = [(0, 7), (7, KT - 7)]


class Unit:

    def __init__(self, reg, c):
        self.reg, self.c = reg, c
        self.g = c % HKV

    def at(self, d):
        return Unit(self.reg, self.c + d)

    def count(self, k, off=0):
        c = k * self.c + off
        return c if self.reg is None else self.reg * (HKV * k) + c

    def batch(self, k=1, off=0):
        c = k * (self.c // HKV) + off
        return c if self.reg is None else self.reg * k + c

    def is_at_most(self, last):
        return self.reg is not None or self.c <= last

    def is_at_least(self, first):
        return self.reg is not None or self.c >= first


def flamingo_block(nc, x, ctxT, mask, g_x, g_f, wq, wkv, wo2, bias_f, bias_far, gateT, w1, b1T, w2, b2,
                   rope_k, rope_q, ident_in, zero_dram, out):
    F32, F16 = mybir.dt.float32, mybir.dt.float16
    ALU = mybir.AluOpType
    ACT = mybir.ActivationFunctionType
    AX = mybir.AxisListType
    ds = bass.ds
    mb_dram = nc.dram_tensor("mask_bias", [B, KP], F16, kind="Internal").ap()
    ctx = ExitStack()
    with ctx:
        def sb(name, shape, dt=F32):
            return ctx.enter_context(nc.sbuf_tensor(name, shape, dt))

        def ps(name, cols):
            return ctx.enter_context(nc.psum_tensor(name, [128, cols], F32))

        def sem(name):
            return ctx.enter_context(nc.semaphore(name))

        X = sb("X", [128, TT, DM])
        WB = sb("WB", [128, H, WIN])
        K1 = sb("K1", [128, HKV, KP], F16)
        K2 = sb("K2", [128, HKV, KP], F16)
        Q1 = sb("Q1", [128, HKV, UC], F16)
        Q2 = sb("Q2", [128, HKV, UC], F16)
        V = sb("V", [128, HKV, KT, D])
        E = sb("E", [128, ERING, UC])
        esum = sb("esum", [128, 2, UC])
        ctx_f = sb("ctx_f", [128, CTX_PARTS[0][1]])
        ctx_hl = sb("ctx_hl", [128, 2, KP], F16)
        kr = sb("kr", [128, KT, D])
        kt1 = sb("kt1", [128, 4, D])
        kt2 = sb("kt2", [128, 4, D])
        khl = sb("khl", [128, KT, 2 * D], F16)
        qr = sb("qr", [128, QT, G, D])
        qt1 = sb("qt1", [128, QT, G, D])
        qt2 = sb("qt2", [128, QT, G, D])
        qhl = sb("qhl", [128, QT, G, 2 * D], F16)
        oraw = sb("oraw", [128, 512])
        rden = sb("rden", [128, 512])
        wkv_hl = sb("wkv_hl", [128, 2, HKV * 2 * D], F16)
        wq_hl = sb("wq_hl", [128, 2, H * D], F16)
        wo_sb = sb("wo_sb", [128, HKV * 2, DM])
        rk = sb("rk", [128, KT, 2, D])
        rkm = sb("rkm", [128, KT, 2, D])
        rq = sb("rq", [128, QT, 2, D])
        xn = sb("xn", [128, TG, DM])
        xnT = sb("xnT", [128, 2, M], F16)
        ident = sb("ident", [128, 128])
        ident16 = sb("ident16", [128, 128], F16)
        ones = sb("ones", [128, 128])
        maskT = sb("maskT", [128, B, KT])
        anyb = sb("anyb", [128, B])
        any16 = sb("any16", [B, 1])
        diag16 = sb("diag16", [B, B])
        far = sb("far", [128, H])
        pm = sb("pm", [128, G * QT, NCH])
        mred = sb("mred", [128, G * QT])
        m16 = sb("m16", [128, G * QT], F16)
        mT = sb("mT", [G * QT, 128], F16)
        junk = sb("junk", [128, 2, 320])
        stats = sb("stats", [128, TT, 6])
        mv = sb("mv", [128, TT, 2])
        std = sb("std", [128, TT])
        rstd = sb("rstd", [128, TT])
        nmr = sb("nmr", [128, TT])
        gx = sb("gx", [128, 2])
        tg_ = sb("tg_", [128, 2])
        gate_sb = sb("gate_sb", [128, NE])
        b1_sb = sb("b1_sb", [128, NE * HC])
        iota_r = sb("iota_r", [128, NE])
        r1 = sb("r1", [128, TT])
        r2 = sb("r2", [128, TT])
        r3 = sb("r3", [128, TT])
        onorm = oraw
        Vf = V[:, :, :, :].rearrange("p g t d -> p (g t d)")
        onerow = Vf[0:1, 0:KP // 2].bitcast(F16)
        bigrow = Vf[0:1, KP // 2:KP // 2 + UC // 2].bitcast(F16)
        mask_u8 = Vf[0:B, 1400:1400 + (S2 + 3) // 4].bitcast(mybir.dt.uint8)[:, 0:S2]
        lg, pr, ga, gb, wsel = (Vf[:, i * TT * NE:(i + 1) * TT * NE].rearrange("p (t e) -> p t e", e=NE)
                                for i in range(5))
        b2_sb = Vf[:, 2048:2048 + NE * DM].rearrange("p (e d) -> p e d", e=NE)
        mask_f = E[0:B, 0:2, :].rearrange("p a c -> p (a c)")[:, 0:KP]
        mask_t = E[0:B, 2:4, :].rearrange("p a c -> p (a c)")[:, 0:KP]
        WBf = WB[:, :, :].rearrange("p h w -> p (h w)")
        NW = NE * HID
        W1f = WBf[:, 0:NW]
        W1h, W1l = (WBf[:, NW:2 * NW].bitcast(F16)[:, i * NW:(i + 1) * NW] for i in range(2))
        W2f = WBf[:, 2 * NW:3 * NW]
        W2h, W2l = (WBf[:, 0:NW].bitcast(F16)[:, i * NW:(i + 1) * NW] for i in range(2))
        XTh = K1[:, :, :].rearrange("p g k -> p (g k)")
        XTl = K2[:, :, :].rearrange("p g k -> p (g k)")
        xn2 = (xn[:, :, :], kr[:, 0:2 * TG, :].rearrange("p (j a) d -> p j (a d)", j=TG))
        hid = E[:, :, :].rearrange("p r c -> p (r c)")
        hid_h = Q1[:, :, :].rearrange("p g c -> p (g c)")
        hid_l = Q2[:, :, :].rearrange("p g c -> p (g c)")
        mb16 = esum[0:B, 0, 0:KP // 2].bitcast(F16)
        wkv_f = oraw[:, :]
        wq_f = esum[:, 1, :]
        oe = esum[:, :, :].rearrange("p a c -> p (a c)")
        xTf = ctx_hl[:, :, :].rearrange("p a k -> p (a k)").bitcast(F32)[:, 0:2 * GC]

        stp = [ps(f"st{i}", UC) for i in range(2)]
        pap = [ps(f"pa{i}", 512) for i in range(2)]
        op = ps("op", 512)
        mp = ps("mp", 512)
        mp16 = mp[:, :].bitcast(F16)
        xt_bank = (mp, pap[1])
        mp_kv = mp[:, :].rearrange("p (t c) -> p t c", t=4)

        names = """mb_out mask_in ident_in kv_in const_in x_in ctx_in mrow_in rows_in bias_in w1_in w2_in b2_in out_done
            init_pool init_dve ident_up mask_f_up mask_ps mask_sb any_up any_ps any_sb mb_up bias_up
            nmr_up tanh_up rkm_up w_hi w_lo ctx_hi ctx_lo xn_up xt_ps xnT_hi xnT_lo kv_ps v_sb k_rope kh_up kl_up
            kt_ps k2_sb k1_sb q_ps q_rope qh_up ql_up qt_ps q2_sb q1_sb
            pa_ps pa_seen pa_max pm_red m16_up mt_ps mT_sb st_ps st_half bias_done e_up pv_ps sum_up o_sb den_ps
            rden_up on_up wo_ps y_up
            ln_stats ln_mv ln_var ln_log ln_rstd w1_hi w1_lo w2_hi w2_lo
            f_xn f_xt_ps f_xhi f_xf f_xlo f_lg_ps f_lg f_max f_sub f_exp f_iota f_gate
            f_h_ps f_gelu f_hi f_lo_pool f_lo_dve f_o_ps f_ob f_y""".split()
        s = {n: sem(n) for n in names}
        mbrow_in = [sem(f"mbrow_in{g}") for g in range(HKV)]
        zrow_in = [sem(f"zrow_in{g}") for g in range(HKV)]
        block = ctx.enter_context(nc.Block())

        N_CONST = 8

        @block.sync
        def _(sp):
            sp.dma_start(mask_u8[:, :], mask).then_inc(s["mask_in"], 16)
            sp.dma_start(ident[:, :], ident_in).then_inc(s["ident_in"], 16)
            sp.dma_start(wkv_f.rearrange("p (g c) -> p g c", g=HKV), wkv).then_inc(s["kv_in"], 16)
            sp.dma_start(rk[:, :, :, :], rope_k).then_inc(s["kv_in"], 16)

            def context_part(b, i):
                k0, n = CTX_PARTS[i]
                sp.dma_start(ctx_f[:, 0:n], ctxT[ds(b, 1), :, k0:k0 + n].rearrange("o d k -> (o d) k"))\
                  .then_inc(s["ctx_in"], 16)

            context_part(0, 0)
            sp.dma_start(X[:, :, :], x.rearrange("b (q p) d -> p (b q) d", p=128)).then_inc(s["x_in"], 16)
            for dst, src in ((far[:, :], bias_far.partition_broadcast(128)), (wq_f, wq), (rq[:, :, :, :], rope_q),
                             (gx[:, 0:1], g_x.partition_broadcast(128)), (gx[:, 1:2], g_f.partition_broadcast(128)),
                             (wo_sb[:, :, :], wo2), (gate_sb[:, :], gateT), (b1_sb[:, :], b1T)):
                sp.dma_start(dst, src).then_inc(s["const_in"], 16)
            sp.wait_ge(s["ctx_lo"], 1)
            context_part(0, 1)
            sp.wait_ge(s["init_pool"], 5)
            for g in range(HKV):
                sp.dma_start(K1[D:D + 1, g, :], onerow[:, :]).then_inc(s["rows_in"], 16)
                sp.dma_start(Q1[D + 1:D + 2, g, :], bigrow[:, :]).then_inc(s["rows_in"], 16)

            def mask_row(P):
                if P.is_at_least(HKV):
                    sp.wait_ge(s["st_ps"], P.count(KT, -3 * KT))
                    sp.dma_start(Q1[D:D + 1, P.g, :], zero_dram).then_inc(zrow_in[P.g], 16)
                sp.dma_start(K1[D + 1:D + 2, P.g, :], mb_dram[ds(P.batch(), 1), :]).then_inc(mbrow_in[P.g], 16)

            def max_row(A):
                sp.wait_ge(s["mT_sb"], A.count(1, 1))
                sp.dma_start(Q1[D:D + 1, A.g, :].rearrange("o (a b) -> o a b", b=128), mT[:, :])\
                  .then_inc(s["mrow_in"], 16)

            def unit(u):
                next_context = u.g == 1 and u.is_at_most(UNITS - 4)
                if next_context:
                    sp.wait_ge(s["ctx_lo"], u.batch(2, 2))
                    context_part(u.batch(1, 1), 0)
                if u.is_at_most(UNITS - 4):
                    mask_row(u.at(3))
                if next_context:
                    sp.wait_ge(s["ctx_lo"], u.batch(2, 3))
                    context_part(u.batch(1, 1), 1)
                if u.is_at_most(UNITS - 2):
                    max_row(u.at(1))

            sp.wait_ge(s["mb_up"], 3)
            sp.dma_start(mb_dram, mb16[:, :]).then_inc(s["mb_out"], 16)
            sp.wait_ge(s["mb_out"], 16)
            for P in range(3):
                mask_row(Unit(None, P))
            sp.dma_start(WB[:, :, :], bass.AP(tensor=bias_f.tensor, offset=bias_f.offset,
                                              ap=[[1, 128], [bias_f.shape[1], H], [1, WIN]])).then_inc(s["bias_in"], 16)
            max_row(Unit(None, 0))
            unit(Unit(None, 0))
            with sp.Fori(0, B - 1) as b:
                for i in range(1, HKV + 1):
                    unit(Unit(b, i))
            unit(Unit(None, UNITS - 3))
            unit(Unit(None, UNITS - 2))
            sp.wait_ge(s["pa_max"], PA * UNITS)
            sp.wait_ge(s["bias_done"], (NEAR + 1) * (UNITS - 2))
            sp.dma_start(W1f.rearrange("p (e h) -> p e h", e=NE), w1.rearrange("e d h -> d e h")).then_inc(s["w1_in"], 16)
            sp.wait_ge(s["bias_done"], (NEAR + 1) * UNITS)
            sp.dma_start(W2f, w2).then_inc(s["w2_in"], 16)
            sp.wait_ge(s["pv_ps"], KT * UNITS)
            sp.dma_start(b2_sb[:, :, :], b2.partition_broadcast(128)).then_inc(s["b2_in"], 16)
            with sp.Fori(0, TT // TG) as t:
                sp.wait_ge(s["f_y"], t * (NE * TG) + NE * TG)
                sp.dma_start(out[ds(t * (TG // QT), TG // QT), :, :].rearrange("b (q p) d -> p (b q) d", p=128),
                             X[:, ds(t * TG, TG), :]).then_inc(s["out_done"], 16)
            sp.wait_ge(s["out_done"], 16 * (TT // TG))

        def mask_rope(e, bt):
            m = maskT[:, ds(bt, 1), :].rearrange("p o t -> p (o t)").unsqueeze(2).broadcast_to([128, KT, 2 * D])
            return e.tensor_tensor(rkm[:, :, :, :].rearrange("p t a d -> p t (a d)"),
                                   rk[:, :, :, :].rearrange("p t a d -> p t (a d)"), m, ALU.mult)

        @block.gpsimd
        def _(pool):
            pool.memset(ctx_hl[:, :, S2:KP], 0.0).then_inc(s["init_pool"], 1)
            for n, (dst, value) in enumerate(((K1[D:128, :, :], 0.0), (Q1[D:128, :, :], 0.0), (onerow, 1.0),
                                              (bigrow, BIG_Q))):
                pool.wait_ge(s["init_pool"], n + 1)
                pool.memset(dst, value).then_inc(s["init_pool"], 1)

            def add(u, t):
                if t == 0:
                    return
                n = KT * u.g + t
                acc = esum[:, u.g % 2, :]
                pool.wait_ge(s["e_up"], u.count(KT, t + 1))
                if t == 1:
                    if u.is_at_least(2):
                        pool.wait_ge(s["den_ps"], u.count(1, -1))
                    pool.tensor_tensor(acc, E[:, (n - 1) % ERING, :], E[:, n % ERING, :], ALU.add)\
                        .then_inc(s["sum_up"], 1)
                else:
                    pool.wait_ge(s["sum_up"], u.count(KT - 1, t - 1))
                    pool.tensor_tensor(acc, acc, E[:, n % ERING, :], ALU.add).then_inc(s["sum_up"], 1)

            def k_low(P, r):
                t0, n = KTR[r]
                pool.wait_ge(s["kh_up"], P.count(2, r + 1))
                pool.tensor_tensor(khl[:, t0:t0 + n, D:2 * D], kr[:, t0:t0 + n, :], khl[:, t0:t0 + n, 0:D],
                                   ALU.subtract).then_inc(s["kl_up"], 1)

            def unit(u):
                for t in range(KT):
                    add(u, t)
                    if t in (7, 9) and u.is_at_most(UNITS - 4):
                        k_low(u.at(3), t // 2 - 3)
                    if t == 0 and u.g == 1 and u.is_at_most(UNITS - 4):
                        pool.wait_ge(s["k_rope"], u.count(16, 48))
                        mask_rope(pool, u.batch(1, 1)).then_inc(s["rkm_up"], 1)

            def relative_bias(g):
                w = WB[:, g * G:(g + 1) * G, :]
                pool.tensor_tensor(w, w, far[:, g * G:(g + 1) * G].unsqueeze(2).broadcast_to([128, G, WIN]),
                                   ALU.subtract).then_inc(s["bias_up"], 1)

            pool.wait_ge(s["const_in"], 16 * N_CONST)
            pool.wait_ge(s["mb_out"], 16)
            pool.wait_ge(s["w_lo"], 2)
            for P in range(3):
                for r in range(2):
                    k_low(Unit(None, P), r)
                if P == 0:
                    pool.wait_ge(s["bias_in"], 16)
                    relative_bias(0)
                relative_bias(P + 1)
            unit(Unit(None, 0))
            with pool.Fori(0, B - 1) as b:
                for i in range(1, HKV + 1):
                    unit(Unit(b, i))
            for i in range(UNITS - 3, UNITS):
                unit(Unit(None, i))

            pool.nop().then_inc(s["f_lo_pool"], 2 * (HC - 1))
            with pool.Fori(0, NG) as t:
                for e in range(NE):
                    for c in range(HC - 1):
                        if c == 0:
                            pool.wait_ge(s["f_o_ps"], t * NE + e + 1)
                        pool.wait_ge(s["f_hi"], t * (NE * HC) + (e + 2) * HC + c + 1)
                        h = slice(((e % 2) * HC + c) * GC, ((e % 2) * HC + c + 1) * GC)
                        pool.tensor_tensor(hid_l[:, h], hid[:, h], hid_h[:, h], ALU.subtract)\
                            .then_inc(s["f_lo_pool"], 1)

        @block.scalar
        def _(act):

            def first_context(i):
                act.wait_ge(s["ctx_in"], 16 * (i + 1))
                k0, n = CTX_PARTS[i]
                act.activation(ctx_hl[:, 0, k0:k0 + n], ctx_f[:, 0:n], ACT.Copy).then_inc(s["ctx_hi"], 1)

            first_context(0)
            act.wait_ge(s["const_in"], 16 * N_CONST)
            act.activation(tg_[:, :], gx[:, :], ACT.Tanh).then_inc(s["tanh_up"], 1)
            act.preload_act_table_set("natural_log_exp_and_others")

            def normalise(bt, n):
                if n is not None:
                    act.wait_ge(s["xt_ps"], n)
                for q in range(QT):
                    last = act.activation(xn[:, q, :], X[:, ds(bt * QT + q, 1), :].rearrange("p o d -> p (o d)"),
                                          ACT.Identity, bias=nmr[:, ds(bt * QT + q, 1)],
                                          scale=rstd[:, ds(bt * QT + q, 1)])
                last.then_inc(s["xn_up"], 1)

            def xt_out(n):
                act.wait_ge(s["xt_ps"], n)
                act.activation(xnT[:, 0, :], mp[:, 0:M], ACT.Copy).then_inc(s["xnT_hi"], 1)

            def context_high(b_in, kv_old, i):
                act.wait_ge(s["ctx_in"], b_in)
                if kv_old is not None:
                    act.wait_ge(s["kv_ps"], kv_old)
                k0, n = CTX_PARTS[i]
                act.activation(ctx_hl[:, 0, k0:k0 + n], ctx_f[:, 0:n], ACT.Copy).then_inc(s["ctx_hi"], 1)

            def kv(P, r):
                t0, n = KV_ROUNDS[r]
                act.wait_ge(s["k_rope"], P.count(16, 4 * r + 3))
                if r == 0 and not P.is_at_least(1):
                    act.wait_ge(s["rows_in"], 16 * 2 * HKV)
                if r == 0 and P.is_at_least(HKV):
                    act.wait_ge(s["pv_ps"], P.count(KT, -3 * KT))
                act.activation(V[:, P.g, t0:t0 + n, :], mp_kv[:, 0:n, D:2 * D], ACT.Copy, scale=1.0 / SW).then_inc(s["v_sb"], 1)

            def k_high(P, r):
                t0, n = KTR[r]
                act.wait_ge(s["k_rope"], P.count(16, 8 * r + 8))
                if r == 0 and P.is_at_least(1):
                    act.wait_ge(s["kt_ps"], P.count(2))
                act.activation(khl[:, t0:t0 + n, 0:D], kr[:, t0:t0 + n, :], ACT.Copy).then_inc(s["kh_up"], 1)

            def q_high(P):
                act.wait_ge(s["q_rope"], P.count(4, 4))
                if P.is_at_least(1):
                    act.wait_ge(s["qt_ps"], P.count(1))
                act.activation(qhl[:, :, :, D:2 * D], qr[:, :, :, :], ACT.Copy).then_inc(s["qh_up"], 1)

            def k_out(P, r):
                t0, n = KTR[r]
                act.wait_ge(s["kt_ps"], P.count(2, r + 1))
                if r == 0 and P.is_at_least(HKV):
                    act.wait_ge(s["st_ps"], P.count(KT, -3 * KT))
                act.activation(K1[0:D, P.g, t0 * 128:(t0 + n) * 128], mp16[0:D, 0:n * 128], ACT.Copy)\
                   .then_inc(s["k1_sb"], 1)
                act.activation(K2[:, P.g, t0 * 128:(t0 + n) * 128], mp16[:, 0:n * 128], ACT.Copy)\
                   .then_inc(s["k2_sb"], 1)

            def q_out(P):
                act.wait_ge(s["qt_ps"], P.count(1, 1))
                act.activation(Q1[0:D, P.g, :], mp16[D:2 * D, 0:UC], ACT.Copy).then_inc(s["q1_sb"], 1)
                act.activation(Q2[:, P.g, :], mp16[:, 0:UC], ACT.Copy).then_inc(s["q2_sb"], 1)

            def exp(u, t):
                n = KT * u.g + t
                if t < NEAR:
                    act.wait_ge(s["bias_done"], u.count(NEAR + 1, t + 2))
                else:
                    act.wait_ge(s["st_ps"], u.count(KT, t + 1))
                if not (u.reg is None and u.c == 0 and t < ERING):
                    act.wait_ge(s["pv_ps"], u.count(KT, t - ERING + 1))
                    k = t - ERING
                    off = max(k, 1) if k >= 0 else k + KT - (KT - 1)
                    act.wait_ge(s["sum_up"], u.count(KT - 1, off))
                act.activation(E[:, n % ERING, :], stp[n % 2][:, :], ACT.Exp).then_inc(s["e_up"], 1)

            def o_out(u):
                act.wait_ge(s["pv_ps"], u.count(KT, KT))
                if u.is_at_least(1):
                    act.wait_ge(s["wo_ps"], u.count(1))
                act.activation(oraw[:, :], op[:, :], ACT.Copy).then_inc(s["o_sb"], 1)

            def prep_round(P, r):
                if r < 4:
                    kv(P, r)
                if r in (2, 4):
                    k_high(P, r // 2 - 1)
                if r == 5:
                    q_high(P)
                if r in (5, 6):
                    k_out(P, r - 5)
                if r == 7:
                    q_out(P)

            def den(u):
                act.wait_ge(s["den_ps"], u.count(1, 1))
                if u.is_at_least(1):
                    act.wait_ge(s["on_up"], u.count(1))
                act.activation(rden[:, :], mp[:, :], ACT.Ln, scale=SUM_UNIT).then_inc(s["rden_up"], 1)
                act.wait_ge(s["rden_up"], u.count(2, 1))
                act.activation(rden[:, :], rden[:, :], ACT.Exp, scale=-1.0).then_inc(s["rden_up"], 1)

            def unit(u):
                P = u.at(3)
                prep = u.is_at_most(UNITS - 4)
                for t in range(KT):
                    if t == KT - 1:
                        o_out(u)
                    next_x = t == 0 and u.g == 1 and prep
                    if next_x:
                        normalise(u.batch(1, 1), u.batch(1, 1))
                    if t + 1 < KT:
                        exp(u, t + 1)
                    elif u.is_at_most(UNITS - 2):
                        exp(u.at(1), 0)
                    if next_x:
                        xt_out(u.batch(1, 2))
                    if t in (0, 3) and u.g == 1 and prep:
                        context_high(u.batch(32, 48 + 16 * (t > 0)), u.count(4, 12), int(t > 0))
                    if t == 1 and u.is_at_least(1):
                        den(u.at(-1))
                    if prep:
                        if 4 <= t < 12:
                            prep_round(P, t - 4)
                    if u.reg is None and u.c == UNITS - 2 and t == 9:
                        rstd_of(0, TT - QT, 3)
                    if u.reg is None and u.c == UNITS - 1 and 5 <= t < 5 + NG - 1:
                        tokens_out(t - 5)
                    if u.reg is None and u.c == UNITS - 1 and 9 <= t:
                        w2_high(t - 9)

            def rstd_of(a, b, n):
                act.wait_ge(s["ln_var"], n)
                act.activation(std[:, a:b], std[:, a:b], ACT.Ln).then_inc(s["ln_log"], 1)
                act.wait_ge(s["ln_log"], n)
                act.activation(rstd[:, a:b], std[:, a:b], ACT.Exp, scale=-0.5).then_inc(s["ln_rstd"], 1)

            def tokens_out(k):
                act.wait_ge(s["f_xt_ps"], k + 1)
                act.activation(XTh[:, k * GC:(k + 1) * GC], xt_bank[k % 2][:, :], ACT.Copy).then_inc(s["f_xhi"], 1)
                if k >= 2:
                    act.wait_ge(s["f_lg_ps"], k - 1)
                act.activation(xTf[:, (k % 2) * GC:(k % 2 + 1) * GC], xt_bank[k % 2][:, :], ACT.Copy)\
                   .then_inc(s["f_xf"], 1)

            def gate_exp(a, b, n):
                act.wait_ge(s["f_sub"], n)
                act.activation(pr[:, a:b, :], lg[:, a:b, :], ACT.Exp).then_inc(s["f_exp"], 1)

            def w2_high(q):
                if q == 0:
                    act.wait_ge(s["w1_lo"], NE // 2)
                    act.wait_ge(s["w2_in"], 16)
                c = slice(q * 2 * HID, (q + 1) * 2 * HID)
                act.activation(W2h[:, c], W2f[:, c], ACT.Copy, scale=SW).then_inc(s["w2_hi"], 1)

            first_context(1)
            rstd_of(0, QT, 1)
            act.wait_ge(s["nmr_up"], 1)
            normalise(0, None)
            xt_out(1)
            for P in range(3):
                for r in range(8):
                    prep_round(Unit(None, P), r)
                if P == 0:
                    rstd_of(QT, TT, 2)
                    act.wait_ge(s["nmr_up"], 2)
            exp(Unit(None, 0), 0)
            unit(Unit(None, 0))
            with act.Fori(0, B - 1) as b:
                for i in range(1, HKV + 1):
                    unit(Unit(b, i))
            for i in range(UNITS - 3, UNITS):
                unit(Unit(None, i))

            act.nop().then_inc(s["f_gelu"], HC)
            den(Unit(None, UNITS - 1))
            gate_exp(0, TT - TG, 1)
            rstd_of(TT - QT, TT, 4)
            tokens_out(NG - 1)
            gate_exp(TT - TG, TT, 2)
            with act.Fori(0, NG) as t:
                for e in range(NE):
                    act.wait_ge(s["f_hi"], t * (NE * HC) + (e + 1) * HC)
                    act.wait_ge(s["f_lo_pool"], t * (NE * (HC - 1)) + (e + 1) * (HC - 1))
                    act.wait_ge(s["f_lo_dve"], t * NE + e + 1)
                    for c in range(HC):
                        k = e * HC + c
                        act.wait_ge(s["f_h_ps"], t * (NE * HC) + k + 1)
                        act.activation(hid[:, ((e % 2) * HC + c) * GC:((e % 2) * HC + c + 1) * GC],
                                       stp[k // 2 % 2][:, GC * (k % 2):GC * (k % 2) + GC], ACT.Gelu,
                                       bias=b1_sb[:, k:k + 1], scale=1.0 / SW).then_inc(s["f_gelu"], 1)

        @block.tensor
        def _(pe):
            pe.wait_ge(s["ident_in"], 16)
            pe.wait_ge(s["ident_up"], 1)
            pe.wait_ge(s["init_dve"], 1)
            pe.wait_ge(s["mask_f_up"], 2)
            for t in range(KT):
                last = pe.transpose(mp[:, t * B:(t + 1) * B], mask_f[:, t * 128:(t + 1) * 128], ident[0:B, 0:B])
            last.then_inc(s["mask_ps"], 1)
            pe.wait_ge(s["mask_sb"], 1)
            pe.wait_ge(s["any_up"], 2)
            pe.matmul(mp[:, 0:B], ones[0:B, :], diag16[:, :], start=True, stop=True).then_inc(s["any_ps"], 1)
            pe.wait_ge(s["any_sb"], 1)

            def xt(b_sem):
                pe.wait_ge(s["xn_up"], b_sem)
                for q in range(QT):
                    last = pe.transpose(mp[:, q * 128:(q + 1) * 128], xn[:, q, :], ident[:, :])
                last.then_inc(s["xt_ps"], 1)

            def kv(P, r):
                t0, n = KV_ROUNDS[r]
                if r:
                    pe.wait_ge(s["v_sb"], P.count(4, r))
                    pe.wait_ge(s["k_rope"], P.count(16, 4 * r - 1))
                if r < 2:
                    pe.wait_ge(s["ctx_hi"], P.batch(2, r + 1))
                    pe.wait_ge(s["ctx_lo"], P.batch(2, r + 1))
                w = slice(P.g * 2 * D, (P.g + 1) * 2 * D)
                for j in range(n):
                    k = slice((t0 + j) * 128, (t0 + j + 1) * 128)
                    pe.matmul(mp_kv[:, j, :], ctx_hl[:, 0, k], wkv_hl[:, 0, w], start=True, stop=False)
                    pe.matmul(mp_kv[:, j, :], ctx_hl[:, 0, k], wkv_hl[:, 1, w], start=False, stop=False)
                    last = pe.matmul(mp_kv[:, j, :], ctx_hl[:, 1, k], wkv_hl[:, 0, w], start=False, stop=True)
                last.then_inc(s["kv_ps"], 1)

            def q_proj(P):
                pe.wait_ge(s["v_sb"], P.count(4, 4))
                pe.wait_ge(s["k_rope"], P.count(16, 15))
                pe.wait_ge(s["xnT_hi"], P.batch(1, 1))
                pe.wait_ge(s["xnT_lo"], P.batch(1, 1))
                w = slice(P.g * G * D, (P.g + 1) * G * D)
                for q in range(QT):
                    o, c = mp[:, q * 256:(q + 1) * 256], slice(q * 128, (q + 1) * 128)
                    pe.matmul(o, xnT[:, 0, c], wq_hl[:, 0, w], start=True, stop=False)
                    pe.matmul(o, xnT[:, 0, c], wq_hl[:, 1, w], start=False, stop=False)
                    last = pe.matmul(o, xnT[:, 1, c], wq_hl[:, 0, w], start=False, stop=True)
                last.then_inc(s["q_ps"], 1)

            def k_turn(P, r):
                t0, n = KTR[r]
                if r:
                    pe.wait_ge(s["k2_sb"], P.count(2, 1))
                    pe.wait_ge(s["k1_sb"], P.count(2, 1))
                else:
                    pe.wait_ge(s["q_rope"], P.count(4, 3))
                pe.wait_ge(s["kh_up"], P.count(2, r + 1))
                pe.wait_ge(s["kl_up"], P.count(2, r + 1))
                for j in range(n):
                    last = pe.transpose(mp16[:, j * 128:(j + 1) * 128], khl[:, t0 + j, :], ident16[:, :])
                last.then_inc(s["kt_ps"], 1)

            def q_turn(P):
                pe.wait_ge(s["k2_sb"], P.count(2, 2))
                pe.wait_ge(s["k1_sb"], P.count(2, 2))
                pe.wait_ge(s["qh_up"], P.count(1, 1))
                pe.wait_ge(s["ql_up"], P.count(1, 1))
                for j in range(G):
                    for q in range(QT):
                        c = (j * QT + q) * 128
                        last = pe.transpose(mp16[:, c:c + 128], qhl[:, q, j, :], ident16[:, :])
                last.then_inc(s["qt_ps"], 1)

            def turned(n):
                pe.wait_ge(s["q1_sb"], n)
                pe.wait_ge(s["q2_sb"], n)

            def chunk(A, i):
                if i == 0:
                    turned(A.count(1, 1))
                    pe.wait_ge(s["k1_sb"], A.count(2, 2))
                    pe.wait_ge(mbrow_in[A.g], A.batch(16, 16))
                    if A.is_at_least(HKV):
                        pe.wait_ge(zrow_in[A.g], A.batch(16))
                    else:
                        pe.wait_ge(s["rows_in"], 16 * 2 * HKV)
                if not (A.reg is None and A.c == 0 and i < 2):
                    pe.wait_ge(s["pa_max"], A.count(PA, i - 1))
                hq, c = divmod(i, NCH)
                k0, n, _ = CHUNKS[c]
                pe.matmul(pap[i % 2][:, 0:n], Q1[:, A.g, hq * 128:(hq + 1) * 128], K1[:, A.g, k0:k0 + n],
                          start=True, stop=True).then_inc(s["pa_ps"], 1)

            def m_turn(A):
                pe.wait_ge(s["m16_up"], A.count(1, 1))
                pe.transpose(mp16[0:G * QT, 0:128], m16[:, :], ident16[:, :]).then_inc(s["mt_ps"], 1)

            def scores(u, t, hf):
                n = KT * u.g + t
                if t == 0 and hf == 0:
                    pe.wait_ge(s["mrow_in"], u.count(16, 16))
                    pe.wait_ge(s["k2_sb"], u.count(2, 2))
                if hf == 0 and not (u.reg is None and u.c == 0 and t < 2):
                    pe.wait_ge(s["e_up"], u.count(KT, t - 1))
                cols = slice(hf * 512, hf * 512 + 512)
                pe.matmul(stp[n % 2][:, cols], K1[:, u.g, t * 128:(t + 1) * 128], Q1[:, u.g, cols],
                          start=True, stop=False)
                last = pe.matmul(stp[n % 2][:, cols], K2[:, u.g, t * 128:(t + 1) * 128], Q2[:, u.g, cols],
                                 start=False, stop=True)
                if hf == 1:
                    last.then_inc(s["st_ps"], 1)
                elif t == 0:
                    last.then_inc(s["st_half"], 1)

            def pv(u, t):
                n = KT * u.g + t
                pe.wait_ge(s["e_up"], u.count(KT, t + 1))
                if t == 0 and u.is_at_least(1):
                    pe.wait_ge(s["o_sb"], u.count(1))
                for hf in range(2):
                    last = pe.matmul(op[hf * 64:hf * 64 + 64, :], V[:, u.g, t, :],
                                     E[:, n % ERING, hf * 512:hf * 512 + 512], start=(t == 0), stop=(t == KT - 1))
                last.then_inc(s["pv_ps"], 1)

            def den(u):
                pe.wait_ge(s["sum_up"], u.count(KT - 1, KT - 1))
                for hf in range(2):
                    last = pe.matmul(mp[hf * 64:hf * 64 + 64, :], ones[:, 0:64],
                                     esum[:, u.g % 2, hf * 512:hf * 512 + 512], start=True, stop=True)
                last.then_inc(s["den_ps"], 1)

            def out_proj(u):
                pe.wait_ge(s["on_up"], u.count(1, 1))
                for q in range(QT):
                    for hh in range(2):
                        last = pe.matmul(mp[:, q * 128:(q + 1) * 128],
                                         onorm[:, hh * 256 + q * 128:hh * 256 + (q + 1) * 128],
                                         wo_sb[:, u.g * 2 + hh, :], start=(hh == 0), stop=(hh == 1))
                last.then_inc(s["wo_ps"], 1)

            def prep_round(P, r):
                if r < 4:
                    kv(P, r)
                if r == 4:
                    q_proj(P)
                if r in (5, 6):
                    k_turn(P, r - 5)
                if r == 7:
                    q_turn(P)

            def unit(u):
                P, A = u.at(3), u.at(2)
                prep, passa = u.is_at_most(UNITS - 4), u.is_at_most(UNITS - 3)
                for t in range(KT):
                    for hf in range(2):
                        if passa and hf < PA_STEPS[t]:
                            chunk(A, PA_FROM[t] + hf)
                        if t + 1 < KT:
                            scores(u, t + 1, hf)
                        elif u.is_at_most(UNITS - 2):
                            scores(u.at(1), 0, hf)
                    if passa:
                        for i in range(PA_FROM[t] + 2, PA_FROM[t + 1]):
                            chunk(A, i)
                    late_den = t == 1 and u.g == 1 and prep
                    if late_den:
                        pv(u, t)
                    if t == 1 and u.is_at_least(1):
                        if u.is_at_most(UNITS - 3):
                            turned(P.count(1))
                        if late_den:
                            pe.wait_ge(s["xnT_lo"], u.batch(1, 2))
                        if u.is_at_least(2):
                            pe.wait_ge(s["y_up"], u.count(1, -1))
                        den(u.at(-1))
                    if t == 2 and u.is_at_most(UNITS - 2):
                        if u.is_at_least(1):
                            pe.wait_ge(s["rden_up"], u.count(2, -1))
                        else:
                            turned(3)
                        m_turn(u.at(1))
                    if t == 3 and u.is_at_least(1):
                        if u.is_at_most(UNITS - 2):
                            pe.wait_ge(s["mT_sb"], u.count(1, 2))
                        else:
                            pe.wait_ge(s["rden_up"], u.count(2, -1))
                        out_proj(u.at(-1))
                    if prep:
                        if t == 4:
                            if u.is_at_least(1):
                                pe.wait_ge(s["y_up"], u.count(1))
                            else:
                                pe.wait_ge(s["mT_sb"], 2)
                        if 4 <= t < 12:
                            prep_round(P, t - 4)
                    if not late_den:
                        pv(u, t)
                    if t == 0 and u.g == 1 and prep:
                        turned(P.count(1))
                        xt(u.batch(1, 2))
                    if u.reg is None and u.c == UNITS - 1:
                        if 5 <= t < 5 + NG - 1:
                            tokens_turn(t - 5)
                        if 6 <= t < 6 + NG - 1:
                            gate_logits(t - 6)

            def tokens_turn(k):
                pe.wait_ge(s["f_xn"], k + 1)
                if k >= 2:
                    pe.wait_ge(s["f_xlo"], k - 1)
                for j in range(TG):
                    last = pe.transpose(xt_bank[k % 2][:, j * 128:(j + 1) * 128], xn2[k % 2][:, j, :], ident[:, :])
                last.then_inc(s["f_xt_ps"], 1)

            def gate_logits(k):
                pe.wait_ge(s["f_xf"], k + 1)
                for j in range(TG):
                    a, c = (k % 2) * GC + j * 128, (k * TG + j) * NE
                    last = pe.matmul(pap[0][:, c:c + NE], xTf[:, a:a + 128], gate_sb[:, :], start=True, stop=True)
                last.then_inc(s["f_lg_ps"], 1)

            xt(1)
            pe.wait_ge(s["xnT_lo"], 1)
            pe.wait_ge(s["const_in"], 16 * N_CONST)
            pe.wait_ge(s["w_hi"], 2)
            pe.wait_ge(s["w_lo"], 2)
            for P in range(3):
                for r in range(8):
                    if P:
                        for i in range(4 * r, 4 * r + 2):
                            chunk(Unit(None, P - 1), i)
                    if r == 0 and P == 1:
                        turned(1)
                    if r == 0 and P == 2:
                        pe.wait_ge(s["mT_sb"], 1)
                    prep_round(Unit(None, P), r)
                    if P:
                        for i in range(4 * r + 2, 4 * r + 4):
                            chunk(Unit(None, P - 1), i)
                if P == 1:
                    turned(2)
                    m_turn(Unit(None, 0))
            scores(Unit(None, 0), 0, 0)
            scores(Unit(None, 0), 0, 1)
            unit(Unit(None, 0))
            with pe.Fori(0, B - 1) as b:
                for i in range(1, HKV + 1):
                    unit(Unit(b, i))
            for i in range(UNITS - 3, UNITS):
                unit(Unit(None, i))
            last_u = Unit(None, UNITS - 1)
            pe.wait_ge(s["y_up"], UNITS - 1)
            pe.wait_ge(s["f_xlo"], NG - 1)
            den(last_u)

            def up(t, e):
                xc = ds(t * GC, GC)
                for c in range(HC):
                    k = e * HC + c
                    wc = slice(k * 128, (k + 1) * 128)
                    pe.wait_ge(s["f_gelu"], t * (NE * HC) + k + 1)
                    bank = stp[k // 2 % 2][:, GC * (k % 2):GC * (k % 2) + GC]
                    pe.matmul(bank, W1h[:, wc], XTh[:, xc], start=True, stop=False)
                    pe.matmul(bank, W1h[:, wc], XTl[:, xc], start=False, stop=False)
                    pe.matmul(bank, W1l[:, wc], XTh[:, xc], start=False, stop=True).then_inc(s["f_h_ps"], 1)

            def down(t, e):
                pe.wait_ge(s["f_hi"], t * (NE * HC) + (e + 3) * HC)
                pe.wait_ge(s["f_lo_pool"], t * (NE * (HC - 1)) + (e + 3) * (HC - 1))
                pe.wait_ge(s["f_lo_dve"], t * NE + e + 3)
                pe.wait_ge(s["f_ob"], t * NE + e + 1)
                for j in range(TG):
                    for c in range(HC):
                        a = ((e % 2) * HC + c) * GC + j * 128
                        wc = slice((e * HC + c) * 128, (e * HC + c + 1) * 128)
                        o = pap[e % 2][:, j * 128:(j + 1) * 128]
                        pe.matmul(o, hid_h[:, a:a + 128], W2h[:, wc], start=(c == 0), stop=False)
                        pe.matmul(o, hid_h[:, a:a + 128], W2l[:, wc], start=False, stop=False)
                        last = pe.matmul(o, hid_l[:, a:a + 128], W2h[:, wc], start=False, stop=(c == HC - 1))
                last.then_inc(s["f_o_ps"], 1)

            def group(t, last):
                for e in range(NE):
                    if e + 1 < NE:
                        up(t, e + 1)
                    elif not last:
                        up(t + 1, 0)
                    down(t, e)

            pe.nop().then_inc(s["f_o_ps"], 2)
            pe.wait_ge(s["w1_hi"], 1)
            pe.wait_ge(s["w1_lo"], NE // 2)
            up(0, 0)
            pe.wait_ge(s["rden_up"], 2 * UNITS - 1)
            out_proj(last_u)
            tokens_turn(NG - 1)
            gate_logits(NG - 1)
            pe.wait_ge(s["f_lg"], 2)
            pe.wait_ge(s["w2_hi"], NE // 2)
            pe.wait_ge(s["w2_lo"], NE // 2)
            with pe.Fori(0, NG - 1) as t:
                group(t, False)
            group(NG - 1, True)

        @block.vector
        def _(dve):
            dve.memset(ones[:, :], 1.0).then_inc(s["init_dve"], 1)
            dve.memset(mask_f, 0.0).then_inc(s["mask_f_up"], 1)
            for e in range(NE):
                dve.memset(iota_r[:, e:e + 1], float(NE - e)).then_inc(s["f_iota"], 1)
            dve.memset(mb16[:, S2:KP], BIG_K).then_inc(s["mb_up"], 1)
            dve.wait_ge(s["mask_in"], 16)
            dve.wait_ge(s["mask_f_up"], 1)
            dve.tensor_copy(mask_f[:, 0:S2], mask_u8[:, :]).then_inc(s["mask_f_up"], 1)
            dve.wait_ge(s["mask_f_up"], 2)
            dve.tensor_reduce(any16[:, :], mask_f, AX.X, ALU.max).then_inc(s["any_up"], 1)
            dve.tensor_scalar(mask_t, mask_f, -1.0, -BIG_K, ALU.add, ALU.mult).then_inc(s["mb_up"], 1)
            dve.wait_ge(s["ident_in"], 16)
            dve.tensor_copy(ident16[:, :], ident[:, :]).then_inc(s["ident_up"], 1)
            dve.wait_ge(s["any_up"], 1)
            dve.tensor_scalar(diag16[:, :], ident[0:B, 0:B], any16[:, 0:1], None, ALU.mult).then_inc(s["any_up"], 1)
            dve.wait_ge(s["mb_up"], 2)
            dve.tensor_scalar(mb16[:, 0:S2], mask_t[:, 0:S2], any16[:, 0:1], None, ALU.mult).then_inc(s["mb_up"], 1)
            dve.wait_ge(s["mask_ps"], 1)
            dve.tensor_copy(maskT[:, :, :].rearrange("p b t -> p t b"),
                            mp[:, 0:KT * B].rearrange("p (t b) -> p t b", t=KT)).then_inc(s["mask_sb"], 1)
            dve.wait_ge(s["any_ps"], 1)
            dve.tensor_copy(anyb[:, :], mp[:, 0:B]).then_inc(s["any_sb"], 1)
            def xt_low(n):
                dve.wait_ge(s["xnT_hi"], n)
                dve.tensor_tensor(xnT[:, 1, :], mp[:, 0:M], xnT[:, 0, :], ALU.subtract).then_inc(s["xnT_lo"], 1)

            def context_low(n, i):
                dve.wait_ge(s["ctx_hi"], n)
                k0, w = CTX_PARTS[i]
                dve.tensor_tensor(ctx_hl[:, 1, k0:k0 + w], ctx_f[:, 0:w], ctx_hl[:, 0, k0:k0 + w], ALU.subtract)\
                   .then_inc(s["ctx_lo"], 1)

            def kv(P, r):
                t0, n = KV_ROUNDS[r]
                if r == 0:
                    dve.wait_ge(s["rkm_up"], P.batch(1, 1))
                    if P.is_at_least(1):
                        dve.wait_ge(s["kh_up"], P.count(2))
                        dve.wait_ge(s["kl_up"], P.count(2))
                if not (P.reg is None and P.c == 0 and r == 0):
                    dve.wait_ge(s["k_rope"], P.count(16, 4 * r))
                dve.wait_ge(s["kv_ps"], P.count(4, r + 1))
                h = D // 2
                dve.tensor_tensor(kt1[:, 0:n, :], mp_kv[:, 0:n, 0:D], rkm[:, t0:t0 + n, 0, :], ALU.mult)\
                   .then_inc(s["k_rope"], 1)
                dve.tensor_tensor(kt2[:, 0:n, 0:h], mp_kv[:, 0:n, h:D], rkm[:, t0:t0 + n, 1, 0:h], ALU.mult)\
                   .then_inc(s["k_rope"], 1)
                dve.tensor_tensor(kt2[:, 0:n, h:D], mp_kv[:, 0:n, 0:h], rkm[:, t0:t0 + n, 1, h:D], ALU.mult)\
                   .then_inc(s["k_rope"], 1)
                dve.wait_ge(s["k_rope"], P.count(16, 4 * r + 3))
                dve.tensor_tensor(kr[:, t0:t0 + n, :], kt1[:, 0:n, :], kt2[:, 0:n, :], ALU.add)\
                   .then_inc(s["k_rope"], 1)

            def q_rope(P):
                h = D // 2
                dve.wait_ge(s["q_ps"], P.count(1, 1))
                if P.is_at_least(1):
                    dve.wait_ge(s["q_rope"], P.count(4))
                    dve.wait_ge(s["qh_up"], P.count(1))
                    dve.wait_ge(s["ql_up"], P.count(1))
                m = mp[:, :].rearrange("p (q j d) -> p q j d", q=QT, j=G)
                cos = rq[:, :, 0:1, :].broadcast_to([128, QT, G, D])
                dve.tensor_tensor(qt1[:, :, :, :], m, cos, ALU.mult).then_inc(s["q_rope"], 1)
                dve.tensor_tensor(qt2[:, :, :, 0:h], m[:, :, :, h:D],
                                  rq[:, :, 1:2, 0:h].broadcast_to([128, QT, G, h]), ALU.mult).then_inc(s["q_rope"], 1)
                dve.tensor_tensor(qt2[:, :, :, h:D], m[:, :, :, 0:h],
                                  rq[:, :, 1:2, h:D].broadcast_to([128, QT, G, h]), ALU.mult).then_inc(s["q_rope"], 1)
                dve.wait_ge(s["q_rope"], P.count(4, 3))
                dve.tensor_tensor(qr[:, :, :, :], qt1[:, :, :, :], qt2[:, :, :, :], ALU.add).then_inc(s["q_rope"], 1)

            def q_low(P):
                dve.wait_ge(s["qh_up"], P.count(1, 1))
                dve.tensor_tensor(qhl[:, :, :, 0:D], qr[:, :, :, :], qhl[:, :, :, D:2 * D], ALU.subtract)\
                   .then_inc(s["ql_up"], 1)

            def prep_round(P, r):
                if r < 4:
                    kv(P, r)
                if r == 4:
                    q_rope(P)
                if r == 5:
                    q_low(P)

            def chunk(A, i):
                hq, c = divmod(i, NCH)
                j, q = divmod(hq, QT)
                k0, n, with_bias = CHUNKS[c]
                if i == 0 and A.is_at_least(1):
                    dve.wait_ge(s["pm_red"], A.count(1))
                dve.wait_ge(s["pa_ps"], A.count(PA, i + 1))
                if with_bias:
                    a = 128 * q + k0
                    if not (A.reg is None and A.c == 0 and i < 2):
                        dve.wait_ge(s["pa_max"], A.count(PA, i - 1))
                    dve.sem_inc(s["pa_seen"], 1)
                    dve.tensor_tensor_reduce(junk[:, i % 2, :], pap[i % 2][:, 0:n], WB[:, A.g * G + j, a:a + n], 1.0,
                                             -3.0e38, ALU.add, ALU.max, pm[:, hq, c:c + 1]).then_inc(s["pa_max"], 1)
                else:
                    dve.tensor_reduce(pm[:, hq, c:c + 1], pap[i % 2][:, 0:n], AX.X, ALU.max)\
                       .then_inc(s["pa_max"], 1)

            def maxima(A):
                dve.wait_ge(s["pa_max"], A.count(PA, PA))
                if A.is_at_least(1):
                    dve.wait_ge(s["m16_up"], A.count(1))
                dve.tensor_reduce(mred[:, :], pm[:, :, :], AX.X, ALU.max).then_inc(s["pm_red"], 1)

            def minus_max(A):
                dve.wait_ge(s["pm_red"], A.count(1, 1))
                if A.is_at_least(1):
                    dve.wait_ge(s["mt_ps"], A.count(1))
                dve.tensor_scalar(m16[:, :], mred[:, :], anyb[:, ds(A.batch(), 1)], -1.0, ALU.mult, ALU.mult)\
                   .then_inc(s["m16_up"], 1)

            def m_out(A):
                dve.wait_ge(s["mt_ps"], A.count(1, 1))
                if A.is_at_least(1):
                    dve.wait_ge(s["mrow_in"], A.count(16))
                dve.tensor_copy(mT[:, :], mp16[0:G * QT, 0:128]).then_inc(s["mT_sb"], 1)

            def bias(u, t):
                dve.wait_ge(s["st_ps"], u.count(KT, t + 1))
                bias_cols(u, t, 0, G)

            def bias_cols(u, t, j0, nj):
                n = KT * u.g + t
                p3 = stp[n % 2][:, j0 * M:(j0 + nj) * M].rearrange("p (j i) -> p j i", j=nj)
                dve.scalar_tensor_tensor(p3, WB[:, u.g * G + j0:u.g * G + j0 + nj, t * 128:t * 128 + M],
                                         maskT[:, ds(u.batch(), 1), t:t + 1].rearrange("p o t -> p (o t)"), p3,
                                         ALU.mult, ALU.add).then_inc(s["bias_done"], 1)

            def bias_first(u, hf):
                if hf == 0:
                    dve.wait_ge(s["st_half"], u.count(1, 1))
                else:
                    dve.wait_ge(s["st_ps"], u.count(KT, 1))
                bias_cols(u, 0, hf * (G // 2), G // 2)

            def den(u):
                dve.wait_ge(s["rden_up"], u.count(2, 2))
                dve.wait_ge(s["o_sb"], u.count(1, 1))
                dve.tensor_tensor(onorm[:, :], oraw[:, :], rden[:, :], ALU.mult).then_inc(s["on_up"], 1)

            def residual(u):
                dve.wait_ge(s["wo_ps"], u.count(1, 1))
                if u.is_at_least(1):
                    dve.wait_ge(s["y_up"], u.count(1))
                xs = X[:, ds(u.batch(QT), QT), :].rearrange("p q d -> p (q d)")
                dve.scalar_tensor_tensor(xs, mp[:, 0:M], tg_[:, 0:1], xs, ALU.mult, ALU.add).then_inc(s["y_up"], 1)

            def unit(u):
                P, A = u.at(3), u.at(2)
                prep, passa = u.is_at_most(UNITS - 4), u.is_at_most(UNITS - 3)
                for t in range(KT):
                    first = min(2, PA_STEPS[t])
                    follows = u.is_at_most(UNITS - 2)
                    for i in range(first):
                        if passa:
                            chunk(A, PA_FROM[t] + i)
                        if t == KT - 1 and i == 0 and follows:
                            bias_first(u.at(1), 0)
                    if t == 1 and u.g == 1 and prep:
                        xt_low(u.batch(1, 2))
                    if t + 1 < NEAR:
                        bias(u, t + 1)
                    if t == KT - 1 and follows:
                        bias_first(u.at(1), 1)
                    if t == 0 and u.is_at_least(1) and follows:
                        minus_max(u.at(1))
                    if t in (1, 4) and u.g == 1 and prep:
                        context_low(u.batch(2, 3 + t // 4), t // 4)
                    if t == 2 and u.is_at_least(1):
                        den(u.at(-1))
                    if passa:
                        for i in range(PA_FROM[t] + first, PA_FROM[t + 1]):
                            chunk(A, i)
                    if t == 2 and u.is_at_most(UNITS - 2):
                        m_out(u.at(1))
                    if t == 3 and u.is_at_least(1):
                        residual(u.at(-1))
                    if prep:
                        if 4 <= t < 12:
                            prep_round(P, t - 4)
                    if t == 12 and passa:
                        maxima(A)
                    if u.reg is None and u.c == UNITS - 2:
                        if t == 5:
                            token_stats(0, TT - QT)
                        if t == 8:
                            token_var(0, TT - QT, TT)
                    if u.reg is None and u.c == UNITS - 1:
                        if t == 0:
                            w1_high()
                        if t in (1, 4):
                            w1_low(t // 2)
                            w1_low(t // 2 + 1)
                        if 4 <= t < 4 + NG - 1:
                            token_norm(t - 4)
                        if 5 <= t < 5 + NG - 1:
                            token_low(t - 5)
                        if t >= 10:
                            w2_low(t - 10)

            def token_stats(a, b):
                for j in range(a, b):
                    dve.bn_stats(stats[:, j, :], X[:, j, :]).then_inc(s["ln_stats"], 1)

            def token_var(a, b, before):
                for j in range(a, b):
                    dve.wait_ge(s["ln_stats"], before + j + 1)
                    dve.bn_aggr(mv[:, j, :], stats[:, j, :]).then_inc(s["ln_mv"], 1)
                dve.wait_ge(s["ln_mv"], before + b)
                dve.tensor_scalar(std[:, a:b], mv[:, a:b, 1], 1e-5, None, ALU.add).then_inc(s["ln_var"], 1)

            def w1_high():
                dve.wait_ge(s["w1_in"], 16)
                dve.wait_ge(s["bias_done"], (NEAR + 1) * (UNITS - 1))
                dve.tensor_scalar(W1h, W1f, SW, None, ALU.mult).then_inc(s["w1_hi"], 1)

            def w1_low(q):
                c = slice(q * 2 * HID, (q + 1) * 2 * HID)
                dve.wait_ge(s["w1_hi"], 1)
                dve.scalar_tensor_tensor(W1l[:, c], W1f[:, c], SW, W1h[:, c], ALU.mult, ALU.subtract)\
                   .then_inc(s["w1_lo"], 1)

            def w2_low(q):
                c = slice(q * 2 * HID, (q + 1) * 2 * HID)
                dve.wait_ge(s["w2_hi"], q + 1)
                dve.scalar_tensor_tensor(W2l[:, c], W2f[:, c], SW, W2h[:, c], ALU.mult, ALU.subtract)\
                   .then_inc(s["w2_lo"], 1)

            def token_norm(k):
                dve.wait_ge(s["ln_rstd"], 3 if k < NG - 1 else 4)
                if k >= 2:
                    dve.wait_ge(s["f_xt_ps"], k - 1)
                for j in range(TG):
                    i = k * TG + j
                    last = dve.tensor_scalar(xn2[k % 2][:, j, :], X[:, i, :], mv[:, i, 0:1], rstd[:, i:i + 1],
                                             ALU.subtract, ALU.mult)
                last.then_inc(s["f_xn"], 1)

            def token_low(k):
                dve.wait_ge(s["f_xhi"], k + 1)
                dve.wait_ge(s["f_xf"], k + 1)
                c = slice(k * GC, (k + 1) * GC)
                dve.tensor_tensor(XTl[:, c], xt_bank[k % 2][:, :], XTh[:, c], ALU.subtract).then_inc(s["f_xlo"], 1)

            def split_weights(h, l, w, n):
                dve.tensor_scalar(h, w, SW, None, ALU.mult).then_inc(s["w_hi"], 1)
                dve.wait_ge(s["w_hi"], n)
                dve.scalar_tensor_tensor(l, w, SW, h, ALU.mult, ALU.subtract).then_inc(s["w_lo"], 1)

            def minus_mean(a, b, n):
                dve.wait_ge(s["ln_rstd"], n)
                dve.scalar_tensor_tensor(nmr[:, a:b], mv[:, a:b, 0], -1.0, rstd[:, a:b], ALU.mult, ALU.mult)\
                   .then_inc(s["nmr_up"], 1)

            dve.wait_ge(s["kv_in"], 32)
            split_weights(wkv_hl[:, 0, :], wkv_hl[:, 1, :], wkv_f, 1)
            context_low(1, 0)
            dve.wait_ge(s["x_in"], 16)
            token_stats(0, QT)
            token_var(0, QT, 0)
            minus_mean(0, QT, 1)
            dve.wait_ge(s["mask_sb"], 1)
            dve.wait_ge(s["kv_in"], 32)
            mask_rope(nc.vector, 0).then_inc(s["rkm_up"], 1)
            context_low(2, 1)
            dve.wait_ge(s["const_in"], 16 * N_CONST)
            split_weights(wq_hl[:, 0, :], wq_hl[:, 1, :], wq_f, 2)
            xt_low(1)
            dve.wait_ge(s["any_sb"], 1)
            dve.wait_ge(s["tanh_up"], 1)
            dve.tensor_scalar(tg_[:, 0:1], tg_[:, 0:1], SUM_UNIT, None, ALU.mult).then_inc(s["tanh_up"], 1)
            dve.wait_ge(s["tanh_up"], 2)
            for P in range(3):
                if P:
                    dve.wait_ge(s["bias_up"], P)
                for r in range(8):
                    if P:
                        for i in range(4 * r, 4 * r + 2):
                            chunk(Unit(None, P - 1), i)
                    prep_round(Unit(None, P), r)
                    if P:
                        for i in range(4 * r + 2, 4 * r + 4):
                            chunk(Unit(None, P - 1), i)
                    if P == 0:
                        token_stats(QT + (TT - QT) * r // 8, QT + (TT - QT) * (r + 1) // 8)
                if P == 0:
                    token_var(QT, TT, 0)
                    minus_mean(QT, TT, 2)
                if P:
                    maxima(Unit(None, P - 1))
                    minus_max(Unit(None, P - 1))
                if P == 1:
                    m_out(Unit(None, 0))
            dve.wait_ge(s["bias_up"], HKV)
            bias_first(Unit(None, 0), 0)
            bias_first(Unit(None, 0), 1)
            unit(Unit(None, 0))
            with dve.Fori(0, B - 1) as b:
                for i in range(1, HKV + 1):
                    unit(Unit(b, i))
            for i in range(UNITS - 3, UNITS):
                unit(Unit(None, i))

            g_count = [0]

            def gate(ins):
                g_count[0] += 1
                ins.then_inc(s["f_gate"], 1)
                dve.wait_ge(s["f_gate"], g_count[0])

            def gate_start(a, b, n):
                def wide(v):
                    return v[:, a:b].unsqueeze(2).broadcast_to([128, b - a, NE])

                dve.wait_ge(s["f_lg_ps"], b // TG)
                dve.tensor_copy(lg[:, a:b, :], pap[0][:, a * NE:b * NE].rearrange("p (t e) -> p t e", e=NE))\
                   .then_inc(s["f_lg"], 1)
                dve.wait_ge(s["f_lg"], n)
                dve.tensor_reduce(r1[:, a:b], lg[:, a:b, :], AX.X, ALU.max).then_inc(s["f_max"], 1)
                dve.wait_ge(s["f_max"], n)
                dve.tensor_tensor(lg[:, a:b, :], lg[:, a:b, :], wide(r1), ALU.subtract).then_inc(s["f_sub"], 1)

            def gate_weights(a, b, n):
                def wide(v):
                    return v[:, a:b].unsqueeze(2).broadcast_to([128, b - a, NE])

                order = iota_r[:, :].unsqueeze(1).broadcast_to([128, b - a, NE])
                p_, w_, a_, b_ = (v[:, a:b, :] for v in (pr, wsel, ga, gb))
                q1, q2, q3 = (v[:, a:b] for v in (r1, r2, r3))

                def first_max(src, sel, best, best_wide):
                    gate(dve.tensor_reduce(best, src, AX.X, ALU.max))
                    gate(dve.tensor_tensor(sel, src, best_wide, ALU.is_equal))
                    gate(dve.tensor_tensor(sel, sel, order, ALU.mult))
                    gate(dve.tensor_reduce(q3, sel, AX.X, ALU.max))
                    gate(dve.tensor_tensor(sel, order, wide(r3), ALU.is_equal))

                dve.wait_ge(s["f_exp"], n)
                gate(dve.tensor_reduce(q1, p_, AX.X, ALU.add))
                gate(dve.reciprocal(q2, q1))
                gate(dve.tensor_tensor(p_, p_, wide(r2), ALU.mult))
                first_max(p_, w_, q1, wide(r1))
                gate(dve.tensor_scalar(a_, w_, -2.0, None, ALU.mult))
                gate(dve.tensor_tensor(a_, a_, p_, ALU.add))
                first_max(a_, b_, q2, wide(r2))
                gate(dve.tensor_tensor(w_, w_, b_, ALU.add))
                gate(dve.tensor_tensor(w_, w_, p_, ALU.mult))
                gate(dve.scalar_tensor_tensor(q3, q1, 1e-9, q2, ALU.add, ALU.add))
                gate(dve.reciprocal(q1, q3))
                gate(dve.tensor_tensor(w_, w_, wide(r1), ALU.mult))
                gate(dve.tensor_scalar(w_, w_, tg_[:, 1:2], None, ALU.mult))

            def hidden_parts(t, e):
                for c in range(HC):
                    h = slice(((e % 2) * HC + c) * GC, ((e % 2) * HC + c + 1) * GC)
                    if c == 0:
                        dve.wait_ge(s["f_o_ps"], t * NE + e + 1)
                    dve.wait_ge(s["f_gelu"], t * (NE * HC) + (e + 1) * HC + c + 1)
                    dve.tensor_copy(hid_h[:, h], hid[:, h]).then_inc(s["f_hi"], 1)
                dve.wait_ge(s["f_hi"], t * (NE * HC) + (e + 3) * HC)
                dve.tensor_tensor(hid_l[:, h], hid[:, h], hid_h[:, h], ALU.subtract).then_inc(s["f_lo_dve"], 1)

            def expert_out(t, e):
                dve.wait_ge(s["f_o_ps"], t * NE + e + 3)
                o = oe[:, (e % 2) * GC:(e % 2 + 1) * GC].rearrange("p (j d) -> p j d", j=TG)
                b2e = b2_sb[:, e:e + 1, :].broadcast_to([128, TG, DM])
                dve.scalar_tensor_tensor(o, pap[e % 2][:, :].rearrange("p (j d) -> p j d", j=TG), 1.0 / SW, b2e,
                                         ALU.mult, ALU.add).then_inc(s["f_ob"], 1)
                dve.wait_ge(s["f_ob"], t * NE + e + 3)
                for j in range(TG):
                    xs = X[:, ds(t * TG + j, 1), :].rearrange("p o d -> p (o d)")
                    w = wsel[:, ds(t * TG + j, 1), e:e + 1].rearrange("p o d -> p (o d)")
                    if e:
                        dve.wait_ge(s["f_y"], t * (NE * TG) + (e - 1) * TG + j + 1)
                    dve.scalar_tensor_tensor(xs, o[:, j, :], w, xs, ALU.mult, ALU.add).then_inc(s["f_y"], 1)

            def group(t, last):
                for e in range(NE):
                    if e + 1 < NE:
                        hidden_parts(t, e + 1)
                    elif not last:
                        hidden_parts(t + 1, 0)
                    expert_out(t, e)

            dve.wait_ge(s["pv_ps"], KT * (UNITS - 2))
            gate_start(0, TT - TG, 1)
            w2_low(NE // 2 - 1)
            last_u = Unit(None, UNITS - 1)
            den(last_u)
            gate_weights(0, TT - TG, 1)
            residual(last_u)
            dve.wait_ge(s["y_up"], UNITS)
            token_stats(TT - QT, TT)
            token_var(TT - QT, TT, TT)
            token_norm(NG - 1)
            token_low(NG - 1)
            gate_start(TT - TG, TT, 2)
            dve.nop().then_inc(s["f_hi"], 2 * HC)
            dve.nop().then_inc(s["f_lo_dve"], 2)
            dve.nop().then_inc(s["f_ob"], 2)
            dve.wait_ge(s["b2_in"], 16)
            hidden_parts(0, 0)
            with dve.Fori(0, NG - 1) as t:
                group(t, False)
            gate_weights(TT - TG, TT, 2)
            group(NG - 1, True)


def _constants():
    import numpy as np
    inv = np.float32(1) / (np.float64(10000.0) ** (np.arange(0, D, 2, dtype=np.float32) / np.float32(D)).astype(np.float64)).astype(np.float32)

    def table(pos, scale):
        f = np.repeat(np.outer(pos.astype(np.float32), inv), 2, axis=-1)
        cos, sin = np.cos(f), np.sin(f)
        sin[:, :D // 2] *= -1
        return (np.stack([cos, sin], 1) * np.float32(scale / SW)).astype(np.float32)

    rk = table(np.arange(KP), 1.0).reshape(KT, 128, 2, D).transpose(1, 0, 2, 3)
    rq = table(M - 1 - np.arange(M), D ** -0.5).reshape(QT, 128, 2, D).transpose(1, 0, 2, 3)
    return np.ascontiguousarray(rk), np.ascontiguousarray(rq), np.eye(128, dtype=np.float32)


def kernel(x, ctx_1024, mask_BxS2_bf1, g_xattn, g_ffn, L0_xattn_Wq, L0_xattn_Wk, L0_xattn_Wv, L0_xattn_Wo,
           L0_xattn_rel_pos_bias, L0_ffn_gate_w, L0_ffn_w1, L0_ffn_b1, L0_ffn_w2, L0_ffn_b2):
    import numpy as np
    import concourse.bacc as bacc
    from concourse.bass_utils import run_bass_kernel_spmd

    a = np.asarray
    c = np.ascontiguousarray
    rk, rq, eye = _constants()
    wk, wv, wo, bias = a(L0_xattn_Wk), a(L0_xattn_Wv), a(L0_xattn_Wo), a(L0_xattn_rel_pos_bias)
    wkv = np.concatenate([wk.reshape(DM, HKV, D), wv.reshape(DM, HKV, D)], axis=2)
    wo2 = wo.reshape(HKV, 2, 2, D, DM).transpose(1, 3, 0, 2, 4).reshape(128, HKV * 2, DM)
    dist = np.minimum(np.abs(np.arange(WIN + 127) - (M - 1)), MAXREL - 1)
    arrays = {
        "x": c(a(x)[:, ::-1, :]), "ctxT": c(a(ctx_1024).transpose(0, 2, 1)), "mask": c(a(mask_BxS2_bf1)).view(np.uint8),
        "g_x": c(a(g_xattn)), "g_f": c(a(g_ffn)), "wq": c(a(L0_xattn_Wq)), "wkv": c(wkv), "wo2": c(wo2),
        "bias_f": c(bias[:, dist]), "bias_far": c(bias[:, MAXREL - 1]), "gateT": c(a(L0_ffn_gate_w).T),
        "w1": c(a(L0_ffn_w1)), "b1T": c(a(L0_ffn_b1).reshape(NE * HC, 128).T),
        "w2": c(a(L0_ffn_w2).reshape(NE * HC, 128, DM).transpose(1, 0, 2).reshape(128, NE * HC * DM)), "b2": c(a(L0_ffn_b2)),
        "rope_k": rk, "rope_q": rq, "ident": eye,
        "zeros": np.zeros((1, UC), np.float16),
    }
    nc = bacc.Bacc("TRN2", target_bir_lowering=False, num_devices=1)
    args = [nc.dram_tensor(f"in_{k}", v.shape, mybir.dt.from_np(v.dtype), kind="ExternalInput").ap()
            for k, v in arrays.items()]
    out = nc.dram_tensor("out_0", [B, M, DM], mybir.dt.float32, kind="ExternalOutput").ap()
    flamingo_block(nc, *args, out)
    r = run_bass_kernel_spmd(nc, [{f"in_{k}": v for k, v in arrays.items()}], core_ids=[0])
    return r.results[0]["out_0"][:, ::-1, :]
```
